# Optimizing a Trainium2 kernel written in Bass

```python
import numpy as np
import jax
import jax.numpy as jnp

def _softmax(x, axis=-1):
    return jax.nn.softmax(x, axis=axis)

def _gelu(x):
    return jax.nn.gelu(x, approximate=True)

def _silu(x):
    return jax.nn.silu(x)

def _sigmoid(x):
    return jax.nn.sigmoid(x)

def _layernorm(x, axis=-1, eps=1e-05):
    m = jnp.mean(x, axis=axis, keepdims=True)
    v = jnp.var(x, axis=axis, keepdims=True)
    return (x - m) / jnp.sqrt(v + eps)

def _scatter_add(tgt, idx, src, axis=0):
    return tgt.at[idx].add(src)

def _segment_sum(src, seg, n):
    return jax.ops.segment_sum(src, seg, n)
kernel_name = 'mk_cond_seq_d2_seqx_r8_7b56f7'

def setup_inputs(seed: int=0):
    np.random.seed(seed)
    _w = jnp.asarray

    def _rec_inputs():
        import jax
        import jax.numpy as jnp
        _rk = jax.random.key(seed)
        x = 7.22e-05 + 1 * jax.random.normal(jax.random.fold_in(_rk, 1), (32, 32, 128), jnp.float32)
        _lenS = 32 - jax.random.randint(jax.random.fold_in(_rk, 7), (32,), 0, max(1, 32 // 4) + 1, jnp.int32)
        _lenS2 = 32 - jax.random.randint(jax.random.fold_in(_rk, 8), (32,), 0, max(1, 32 // 4) + 1, jnp.int32)
        cond_1024 = 0.00782532 + 1.00527 * jax.random.normal(jax.random.fold_in(_rk, 11), (32, 128), jnp.float32)
        _validS = jnp.arange(32)[None, :] < _lenS[:, None]
        _validS2 = jnp.arange(32)[None, :] < _lenS2[:, None]
        _causal = jnp.tril(jnp.ones((32, 32), dtype=bool))
        mask_BxSxSx11_ik0 = jnp.where(jnp.ones((32, 32, 32, 11), dtype=bool), 0, 1).astype(jnp.int32)
        return (x, cond_1024, mask_BxSxSx11_ik0)
    x, cond_1024, mask_BxSxSx11_ik0 = _rec_inputs()

    def _L0_cond_setup():
        import jax, jax.numpy as jnp
        import numpy as np
        EPS = 1e-06

        def _ln(x):
            m = jnp.mean(x, axis=-1, keepdims=True)
            v = jnp.mean(jnp.square(x - m), axis=-1, keepdims=True)
            return (x - m) * jax.lax.rsqrt(v + EPS)

        def _modulate(x, shift, scale):
            return x * (1.0 + scale[:, None]) + shift[:, None]
        key = jax.random.key(seed)
        B, S, H, NH = (8, 128, 128, 16)
        ks = jax.random.split(key, 12)
        s = lambda k, sh: jax.random.normal(k, sh, dtype=jnp.float32) * 0.02
        return {'x': jax.random.normal(ks[0], (B, S, H), dtype=jnp.float32), 'c': jax.random.normal(ks[1], (B, H), dtype=jnp.float32), 'w_ada': s(ks[2], (H, 6 * H)), 'b_ada': jnp.zeros((6 * H,), dtype=jnp.float32), 'w_qkv': s(ks[3], (H, 3 * H)), 'w_proj': s(ks[4], (H, H)), 'b_proj': jnp.zeros((H,), dtype=jnp.float32), 'w_mlp1': s(ks[5], (H, 4 * H)), 'b_mlp1': jnp.zeros((4 * H,), dtype=jnp.float32), 'w_mlp2': s(ks[6], (4 * H, H)), 'b_mlp2': jnp.zeros((H,), dtype=jnp.float32)}
    _L0_cond_all = _L0_cond_setup()
    _L0_cond_in = {k: v for k, v in _L0_cond_all.items() if k in ('w_ada', 'b_ada', 'w_qkv', 'w_proj', 'b_proj', 'w_mlp1', 'b_mlp1', 'w_mlp2', 'b_mlp2')}
    del _L0_cond_all

    def _L1_cond_setup():
        import jax, jax.numpy as jnp
        import numpy as np
        NONGT = 20
        H = 16
        NEG = -9000000000000000.0

        def _gat_attention(self_feat, cond_adj, label_bias, Wq, bq, Wk, bk, Wout, bout):
            B, N, F = self_feat.shape
            ng = min(NONGT, N)
            dh = F // H
            kv = self_feat[:, :ng]
            qh = (self_feat @ Wq.T + bq).reshape(B, N, H, dh)
            kh = (kv @ Wk.T + bk).reshape(B, ng, H, dh)
            aff = jnp.einsum('bnhd,bmhd->bnhm', qh, kh) * (1.0 / np.sqrt(dh))
            mask = cond_adj[:, :, None, :] > 0
            aff = jnp.where(mask, aff, NEG) + label_bias[:, :, None, :]
            w = jax.nn.softmax(aff, axis=-1)
            out_t = jnp.einsum('bnhm,bmf->bnhf', w, kv)
            out = jnp.einsum('bnhf,hgf->bnhg', out_t, Wout) + bout.reshape(H, F // H)
            return out.reshape(B, N, F)

        def _forward(v, q, adj, W_self, b_self, w_bias, b_bias, Wq, bq, Wk, bk, Wout, bout):
            adj_f = adj.astype(jnp.float32)
            exp_v = v
            row_zero = exp_v.sum(-1) == 0
            q_exp = jnp.where(row_zero[..., None], 0.0, q[:, None, :])
            vcq = jnp.concatenate([exp_v, q_exp], axis=-1)
            self_feat = vcq @ W_self.T + b_self
            output = self_feat
            for d in range(2):
                A = adj_f if d == 0 else jnp.swapaxes(adj_f, 1, 2)
                A = A[:, :, :NONGT, :]
                cond = A.sum(-1)
                vb = A @ w_bias + b_bias
                output = output + _gat_attention(self_feat, cond, vb, Wq[d], bq[d], Wk[d], bk[d], Wout[d], bout[d])
            rel = jax.nn.relu(output)
            return exp_v + rel
        key = jax.random.key(seed)
        ks = jax.random.split(key, 8)
        B, N, L, F, Q = (32, 36, 11, 128, 128)
        IN = F + Q
        s = 0.02
        return {'v': jax.random.normal(ks[0], (B, N, F), jnp.float32), 'q': jax.random.normal(ks[1], (B, Q), jnp.float32), 'adj': jax.random.randint(ks[2], (B, N, N, L), 0, 2, jnp.int32), 'W_self': jax.random.normal(ks[3], (F, IN), jnp.float32) * s, 'b_self': jnp.zeros((F,), jnp.float32), 'w_bias': jax.random.normal(ks[4], (L,), jnp.float32) * s, 'b_bias': jnp.zeros((), jnp.float32), 'Wq': jax.random.normal(ks[5], (2, F, F), jnp.float32) * s, 'bq': jnp.zeros((2, F), jnp.float32), 'Wk': jax.random.normal(ks[6], (2, F, F), jnp.float32) * s, 'bk': jnp.zeros((2, F), jnp.float32), 'Wout': jax.random.normal(ks[7], (2, H, F // H, F), jnp.float32) * s, 'bout': jnp.zeros((2, F), jnp.float32)}
    _L1_cond_all = _L1_cond_setup()
    _L1_cond_in = {k: v for k, v in _L1_cond_all.items() if k in ('W_self', 'b_self', 'w_bias', 'b_bias', 'Wq', 'bq', 'Wk', 'bk', 'Wout', 'bout')}
    del _L1_cond_all
    return {'x': x, 'cond_1024': cond_1024, 'mask_BxSxSx11_ik0': mask_BxSxSx11_ik0, 'L0_cond_w_ada': _L0_cond_in['w_ada'], 'L0_cond_b_ada': _L0_cond_in['b_ada'], 'L0_cond_w_qkv': _L0_cond_in['w_qkv'], 'L0_cond_w_proj': _L0_cond_in['w_proj'], 'L0_cond_b_proj': _L0_cond_in['b_proj'], 'L0_cond_w_mlp1': _L0_cond_in['w_mlp1'], 'L0_cond_b_mlp1': _L0_cond_in['b_mlp1'], 'L0_cond_w_mlp2': _L0_cond_in['w_mlp2'], 'L0_cond_b_mlp2': _L0_cond_in['b_mlp2'], 'L1_cond_W_self': _L1_cond_in['W_self'], 'L1_cond_b_self': _L1_cond_in['b_self'], 'L1_cond_w_bias': _L1_cond_in['w_bias'], 'L1_cond_b_bias': _L1_cond_in['b_bias'], 'L1_cond_Wq': _L1_cond_in['Wq'], 'L1_cond_bq': _L1_cond_in['bq'], 'L1_cond_Wk': _L1_cond_in['Wk'], 'L1_cond_bk': _L1_cond_in['bk'], 'L1_cond_Wout': _L1_cond_in['Wout'], 'L1_cond_bout': _L1_cond_in['bout']}

def reference(x, cond_1024, mask_BxSxSx11_ik0, L0_cond_w_ada, L0_cond_b_ada, L0_cond_w_qkv, L0_cond_w_proj, L0_cond_b_proj, L0_cond_w_mlp1, L0_cond_b_mlp1, L0_cond_w_mlp2, L0_cond_b_mlp2, L1_cond_W_self, L1_cond_b_self, L1_cond_w_bias, L1_cond_b_bias, L1_cond_Wq, L1_cond_bq, L1_cond_Wk, L1_cond_bk, L1_cond_Wout, L1_cond_bout):
    import jax
    import jax.numpy as jnp

    def _L0_cond_ref(x, c, w_ada, b_ada, w_qkv, w_proj, b_proj, w_mlp1, b_mlp1, w_mlp2, b_mlp2):
        import jax, jax.numpy as jnp
        import numpy as np
        EPS = 1e-06

        def _ln(x):
            m = jnp.mean(x, axis=-1, keepdims=True)
            v = jnp.mean(jnp.square(x - m), axis=-1, keepdims=True)
            return (x - m) * jax.lax.rsqrt(v + EPS)

        def _modulate(x, shift, scale):
            return x * (1.0 + scale[:, None]) + shift[:, None]
        B, S, H = x.shape
        NH = 16
        CH = H // NH
        cmod = jax.nn.silu(c) @ w_ada + b_ada
        shift_msa, scale_msa, gate_msa, shift_mlp, scale_mlp, gate_mlp = jnp.split(cmod, 6, axis=-1)
        x_mod = _modulate(_ln(x), shift_msa, scale_msa)
        qkv = x_mod @ w_qkv
        k, q, v = jnp.split(qkv, 3, axis=-1)
        k = k.reshape(B, S, NH, CH)
        q = q.reshape(B, S, NH, CH)
        v = v.reshape(B, S, NH, CH)
        q = q / CH
        w = jnp.einsum('bqhc,bkhc->bhqk', q, k).astype(jnp.float32)
        w = jax.nn.softmax(w, axis=-1)
        y = jnp.einsum('bhqk,bkhc->bqhc', w, v).reshape(B, S, H)
        attn_x = y @ w_proj + b_proj
        x = x + gate_msa[:, None] * attn_x
        x_mod2 = _modulate(_ln(x), shift_mlp, scale_mlp)
        h = jax.nn.gelu(x_mod2 @ w_mlp1 + b_mlp1)
        mlp_x = h @ w_mlp2 + b_mlp2
        x = x + gate_mlp[:, None] * mlp_x
        return x

    def _L1_cond_ref(v, q, adj, W_self, b_self, w_bias, b_bias, Wq, bq, Wk, bk, Wout, bout):
        import jax, jax.numpy as jnp
        import numpy as np
        NONGT = 20
        H = 16
        NEG = -9000000000000000.0

        def _gat_attention(self_feat, cond_adj, label_bias, Wq, bq, Wk, bk, Wout, bout):
            B, N, F = self_feat.shape
            ng = min(NONGT, N)
            dh = F // H
            kv = self_feat[:, :ng]
            qh = (self_feat @ Wq.T + bq).reshape(B, N, H, dh)
            kh = (kv @ Wk.T + bk).reshape(B, ng, H, dh)
            aff = jnp.einsum('bnhd,bmhd->bnhm', qh, kh) * (1.0 / np.sqrt(dh))
            mask = cond_adj[:, :, None, :] > 0
            aff = jnp.where(mask, aff, NEG) + label_bias[:, :, None, :]
            w = jax.nn.softmax(aff, axis=-1)
            out_t = jnp.einsum('bnhm,bmf->bnhf', w, kv)
            out = jnp.einsum('bnhf,hgf->bnhg', out_t, Wout) + bout.reshape(H, F // H)
            return out.reshape(B, N, F)

        def _forward(v, q, adj, W_self, b_self, w_bias, b_bias, Wq, bq, Wk, bk, Wout, bout):
            adj_f = adj.astype(jnp.float32)
            exp_v = v
            row_zero = exp_v.sum(-1) == 0
            q_exp = jnp.where(row_zero[..., None], 0.0, q[:, None, :])
            vcq = jnp.concatenate([exp_v, q_exp], axis=-1)
            self_feat = vcq @ W_self.T + b_self
            output = self_feat
            for d in range(2):
                A = adj_f if d == 0 else jnp.swapaxes(adj_f, 1, 2)
                A = A[:, :, :NONGT, :]
                cond = A.sum(-1)
                vb = A @ w_bias + b_bias
                output = output + _gat_attention(self_feat, cond, vb, Wq[d], bq[d], Wk[d], bk[d], Wout[d], bout[d])
            rel = jax.nn.relu(output)
            return exp_v + rel
        return _forward(v, q, adj, W_self, b_self, w_bias, b_bias, Wq, bq, Wk, bk, Wout, bout)
    x = _L0_cond_ref(x, cond_1024, L0_cond_w_ada, L0_cond_b_ada, L0_cond_w_qkv, L0_cond_w_proj, L0_cond_b_proj, L0_cond_w_mlp1, L0_cond_b_mlp1, L0_cond_w_mlp2, L0_cond_b_mlp2)
    x = _L1_cond_ref(x, cond_1024, mask_BxSxSx11_ik0, L1_cond_W_self, L1_cond_b_self, L1_cond_w_bias, L1_cond_b_bias, L1_cond_Wq, L1_cond_bq, L1_cond_Wk, L1_cond_bk, L1_cond_Wout, L1_cond_bout)
    return x

_drawn_inputs = setup_inputs


def setup_inputs(seed=0):
    import zlib

    import numpy as np

    out = dict(_drawn_inputs(seed))
    spreads = {'L0_cond_b_ada': (0.0, 0.545),
     'L0_cond_b_proj': (0.0, 0.476),
     'L0_cond_b_mlp1': (0.0, 0.8),
     'L0_cond_b_mlp2': (0.0, 0.518),
     'L1_cond_b_self': (0.0, 0.401),
     'L1_cond_bq': (0.0, 0.1),
     'L1_cond_bk': (0.0, 0.1),
     'L1_cond_bout': (0.0, 0.276)}
    factors = {'L0_cond_w_ada': 2.906,
     'L0_cond_w_qkv': 8.0,
     'L0_cond_w_proj': 8.0,
     'L0_cond_w_mlp1': 6.171,
     'L0_cond_w_mlp2': 5.651}
    for name, (base, spread) in spreads.items():
        noise = np.random.default_rng([zlib.crc32(name.encode()), seed]).standard_normal(out[name].shape)
        drawn = base * np.exp(spread * noise) if base else spread * noise
        out[name] = jnp.asarray(drawn.astype(out[name].dtype))
    for name, factor in factors.items():
        out[name] = (out[name] * factor).astype(out[name].dtype)
    return out
```

```python
from contextlib import ExitStack

import concourse.bass as bass
from concourse import mybir

ALU = mybir.AluOpType
ACT = mybir.ActivationFunctionType
F32 = mybir.dt.float32
I32 = mybir.dt.int32
AX = mybir.AxisListType

P = 128
B = 32
S = 32
QUAD = 32
HQ = 4
H4 = 4
C = 8
G = 8
UB = 4
HALVES = 2
BH = B // HALVES
UH = G // HALVES
TH = BH * S
M = 20
L = 11
NJ = 4
VW = HQ * C + HQ
LN_EPS = 1e-6
NEG = -9000000000000000.0
DIRS = 2

R_COND = 0
R_ADA = B
R_PROJ = R_ADA + 6
R_MLP1 = R_PROJ + 1
R_MLP2 = R_MLP1 + NJ
R_SELF = R_MLP2 + 1
R_Q = R_SELF + 1
R_K = R_Q + DIRS
R_OUT = R_K + DIRS
ROWS = R_OUT + DIRS

UNITS = [(0, 0, g) for g in range(G)]
for _h in range(HALVES):
    for _d in range(DIRS):
        UNITS += [(1, _d, _h * UH + _u) for _u in range(UH)]
N0 = G


def attention(first, count, dense):
    order = []
    last = first + count
    for s in range(first - 2, last):
        if s + 2 < last:
            order += [("scores", s + 2), ("shift", s + 2)]
        order += dense.get(s - first, [])
        if first <= s + 1 < last:
            order += [("exp", s + 1), ("turn", s + 1)]
        if s >= first:
            order += [("values", s), ("normalise", s)]
    return order


def dense(*names):
    return [("dense", n) for n in names]


def block_tail(h):
    return dense(("yT", h), ("proj", h), ("x1tok", h), ("xn2T", h), ("mlp1", h, 0), ("mlp1", h, 1),
                 ("mlp1", h, 2), ("mlp1", h, 3), ("mlp2", h))


def graph_head(h, d):
    return dense(("q1", h, d), ("k1", h, d), ("v1", h, d))


def graph_self(h):
    return dense(("rowsum", h), ("self", h))


T0, T1 = block_tail(0), block_tail(1)
ORDER = (
    dense("small", "cmod", ("xnT", 0), ("q", 0), ("k", 0), ("v", 0), ("xnT", 1), ("q", 1), ("k", 1), ("v", 1))
    + attention(0, 8, {0: dense("wA", "wB"), 1: dense("qz", ("xT", 0), ("xT", 1)),
                       4: T0[0:2], 5: T0[2:4], 6: T0[4:7], 7: T0[7:9]})
    + graph_self(0) + graph_head(0, 0)
    + attention(8, 16, {-2: graph_head(0, 1), -1: T1[0:2], 0: T1[2:4], 1: T1[4:6], 2: T1[6:8], 3: T1[8:9] + graph_self(1)[0:1],
                        4: graph_self(1)[1:2], 5: graph_head(1, 0), 6: graph_head(1, 1),
                        8: dense(("yfT", 0)), 9: dense(("out", 0))})
    + dense(("yfT", 1), ("out", 1))
)
DENSE = [i for stage, i in ORDER if stage == "dense"]

BY_ACT = {"k", "v", "wA", "wB", "qz", "xT", "yT", "mlp1", "v1", "out"}


def by_act(name):
    if name[0] == "q1":
        return name[2] == 1
    return (name if isinstance(name, str) else name[0]) in BY_ACT


def program(nc, x, cond, adj, w_ada, b_ada, w_qkv, w_proj, b_proj, w_mlp1, b_mlp1, w_mlp2, b_mlp2,
            w_self, b_self, w_bias, b_bias, wq, bq, wk, bk, wout, bout, out):
    with ExitStack() as ctx:
        def sb(name, shape, dt=F32):
            return ctx.enter_context(nc.sbuf_tensor(name, shape, dt))

        def sem(name):
            return ctx.enter_context(nc.semaphore(name))

        ident = sb("ident", [P, P])
        ones = sb("ones", [P, P])
        head_mask = sb("head_mask", [P, 2, H4])
        minus_half = sb("minus_half", [P, UH])
        rows = sb("rows", [64, P])
        cols = sb("cols", [P, ROWS])
        silu_t = sb("silu_t", [P, 2, B])
        silu_c = sb("silu_c", [P, B])
        cmod = sb("cmod", [P, 6, B])
        bout_sum = sb("bout_sum", [P, 1])
        bq_masked = sb("bq_masked", [P, DIRS, H4])
        qz = sb("qz", [P, B])
        x_tok = sb("x_tok", [P, G, P])
        xn_tok = sb("xn_tok", [P, G, P])
        stats = sb("stats", [P, G, 6])
        meanvar = sb("meanvar", [P, G, 2])
        var_eps = sb("var_eps", [P, G])
        rstd = sb("rstd", [P, 2, G])
        xT = sb("xT", [P, B, S])
        xm = sb("xm", [P, B, S])
        xm2 = xm
        gated = sb("gated", [P, B, S])
        x1T = sb("x1T", [P, B, S])
        x2T = sb("x2T", [P, B, S])
        zeroed_q = sb("zeroed_q", [P, BH, S])
        selfT = sb("selfT", [P, B, S])
        hidden = sb("hidden", [P, NJ, TH])
        y_tok = sb("y_tok", [P, G, P])
        yT = sb("yT", [P, B * S])
        y_dir = [yT[:, :].rearrange("p (g f) -> p g f", f=P), y_tok[:, :, :]]
        Qm = [sb(f"Qm{d}", [P, B, H4, S]) for d in range(DIRS)]
        Kz = [sb(f"Kz{d}", [P, B, HQ, S]) for d in range(DIRS)]
        Vz = [sb(f"Vz{d}", [P, B, H4, VW]) for d in range(DIRS)]
        E0 = sb("E0", [P, 3, UB * HQ, S])
        E1 = sb("E1", [P, 3, UB * HQ, S])
        PT = sb("PT", [P, 2, UB, P])
        neg_max = sb("neg_max", [P, 2, UB * HQ])
        rden = sb("rden", [P, 2, H4, HQ])
        w_ada_sb = sb("w_ada_sb", [P, 6 * P])
        w_qkv_sb = sb("w_qkv_sb", [P, 3 * P])
        w_proj_sb = sb("w_proj_sb", [P, P])
        w_mlp1_sb = sb("w_mlp1_sb", [P, NJ * P])
        w_mlp2_sb = sb("w_mlp2_sb", [P, NJ, P])
        w_rows = sb("w_rows", [P, 8, P])
        w_cols = sb("w_cols", [P, 8, P])
        adj_i = Qm[1][:, :, :, :].rearrange("p b h s -> p (b h s)")[:, 0:G * S * L].bitcast(I32)\
            .rearrange("p (g r) -> p g r", g=G)
        adj_f = sb("adj_f", [P, G, S, L])
        wb = sb("wb", [P, L])
        bb = sb("bb", [P, 1])
        label_sum = sb("label_sum", [P, G, S])
        label_bias = sb("label_bias", [P, G, S])
        masked = sb("masked", [P, G, S])
        bias_dir = sb("bias_dir", [P, DIRS, G, S])
        bias_rep = [sb(f"bias_rep{d}", [P, B, M]) for d in range(DIRS)]
        out_tok = x_tok
        outT = x1T
        rT = gated
        W_SELF_X, W_SELF_Q, W_Q, W_K, W_OUT = 0, 1, 2, 4, 6

        def bank(name):
            return ctx.enter_context(nc.psum_tensor(name, [P, 512], F32))
        ps_s = [bank(f"ps_s{i}") for i in range(2)]
        ps_t = [bank(f"ps_t{i}") for i in range(2)]
        ps_y = [bank(f"ps_y{i}") for i in range(2)]
        ps_d = [bank(f"ps_d{i}") for i in range(2)]

        ld = {n: sem("ld_" + n) for n in ("x0", "x1", "rows", "ada", "qkv", "proj", "mlp1", "mlp2", "wrows", "adj", "wb")}
        stored = sem("stored")
        ident_ready = sem("ident_ready")
        consts_ready = sem("consts_ready")
        kz_ready = sem("kz_ready")
        kz1_ready = sem("kz1_ready")
        vz_ready = [sem(f"vz_ready{d}") for d in range(DIRS)]
        dense_ready = sem("dense_ready")
        dense_act = sem("dense_act")
        dense_dve = sem("dense_dve")
        scores_ready = sem("scores_ready")
        scores_read = sem("scores_read")
        shifted = sem("shifted")
        exp_ready = sem("exp_ready")
        turned = sem("turned")
        pt_ready = sem("pt_ready")
        values_ready = sem("values_ready")
        y_ready = sem("y_ready")
        own = sem("own")
        var_ready = sem("var_ready")
        rstd_ready = sem("rstd_ready")
        xn_ready = sem("xn_ready")
        x1_ready = sem("x1_ready")
        x2_ready = sem("x2_ready")
        silu_e = sem("silu_e")
        silu_ready = sem("silu_ready")
        ysum_ready = sem("ysum_ready")
        outT_ready = sem("outT_ready")
        adj_ready = sem("adj_ready")
        labels_ready = sem("labels_ready")
        pool_own = sem("pool_own")
        bias_ready = sem("bias_ready")
        bias_spread = [sem(f"bias_spread{d}") for d in range(DIRS)]

        def taken(name):
            k = DENSE.index(name)
            mine = by_act(name)
            return (dense_act if mine else dense_dve), sum(by_act(n) == mine for n in DENSE[:k + 1])

        def psum_of(name):
            return ps_d[DENSE.index(name) % 2]

        block = ctx.enter_context(nc.Block())

        @block.sync
        def _(sp):
            x_v = x.rearrange("(g b) s f -> (b s) g f", b=UB)
            sp.dma_start(x_tok[:, 0:UH, :], x_v[:, 0:UH, :]).then_inc(ld["x0"], 16)
            sp.dma_start(w_ada_sb[:, :], w_ada).then_inc(ld["ada"], 16)
            sp.dma_start(x_tok[:, UH:G, :], x_v[:, UH:G, :]).then_inc(ld["x1"], 16)
            sp.dma_start(w_rows[:, 0:2, :], w_self.rearrange("o (j i) -> o j i", j=2)).then_inc(ld["wrows"], 16)
            for k, w in ((W_Q, wq), (W_K, wk)):
                sp.dma_start(w_rows[:, k:k + DIRS, :], w.rearrange("d o i -> o d i")).then_inc(ld["wrows"], 16)
            sp.dma_start(w_rows[:, W_OUT:W_OUT + DIRS, :], wout.rearrange("d h g f -> (h g) d f")).then_inc(ld["wrows"], 16)
            sp.dma_start(adj_i[:, :, :], adj.rearrange("(g b) i j l -> (b i) g (j l)", b=UB)).then_inc(ld["adj"], 16)
            sp.dma_start(w_proj_sb[:, :], w_proj).then_inc(ld["proj"], 16)
            sp.dma_start(w_mlp1_sb[:, :], w_mlp1).then_inc(ld["mlp1"], 16)
            sp.dma_start(w_mlp2_sb[:, :, :], w_mlp2.rearrange("(j p) n -> p j n", p=P)).then_inc(ld["mlp2"], 16)
            for d in range(DIRS):
                sp.wait_ge(bias_ready, d + 1)
                for b in range(UB):
                    for h4 in range(H4):
                        sp.dma_start(bias_rep[d][QUAD * h4:QUAD * h4 + QUAD, b:B:UB, :],
                                     bias_dir[QUAD * b:QUAD * b + QUAD, d, :, 0:M]).then_inc(bias_spread[d], 16)
            o_v = out.rearrange("(g b) s f -> (b s) g f", b=UB)
            for h in range(HALVES):
                sp.wait_ge(*taken(("out", h)))
                sp.dma_start(o_v[:, h * UH:(h + 1) * UH, :], out_tok[:, h * UH:(h + 1) * UH, :]).then_inc(stored, 16)
            sp.wait_ge(stored, 16 * HALVES)

        @block.gpsimd
        def _(pool):
            pool.memset(ident[:, :], 0.0).then_inc(pool_own, 1)
            pool.wait_ge(pool_own, 1)
            pool.affine_select(out=ident[:, :], in_=ident[:, :], compare_op=ALU.not_equal, fill=1.0, base=0,
                               pattern=[[-1, P]], channel_multiplier=1).then_inc(ident_ready, 1)
            pool.memset(minus_half[:, :], -0.5).then_inc(pool_own, 1)

            def ones_block(d):
                for hq in range(HQ):
                    pool.memset(Vz[d][QUAD * hq:QUAD * hq + QUAD, :, :, HQ * C + hq], 1.0).then_inc(vz_ready[d], 1)
                pool.wait_ge(vz_ready[d], HQ)

            def rstd_of(layer, h):
                pool.wait_ge(pool_own, 2)
                pool.wait_ge(var_ready, HALVES * layer + h + 1)
                pool.tensor_tensor(rstd[:, layer, h * UH:(h + 1) * UH], var_eps[:, h * UH:(h + 1) * UH],
                                   minus_half[:, :], ALU.pow).then_inc(rstd_ready, 1)

            pool.memset(Vz[0][:, 0:BH, :, :], 0.0).then_inc(pool_own, 1)
            rstd_of(0, 0)
            pool.memset(Vz[0][:, BH:B, :, :], 0.0).then_inc(pool_own, 1)
            pool.wait_ge(pool_own, 4)
            ones_block(0)
            rstd_of(0, 1)
            pool.memset(ones[:, :], 1.0).then_inc(consts_ready, 1)
            pool.memset(Kz[1][:, :, :, :], 0.0).then_inc(kz1_ready, 1)
            pool.memset(Vz[1][:, :, :, :], 0.0).then_inc(pool_own, 1)
            pool.wait_ge(pool_own, 5)
            ones_block(1)

            own_n = 5
            pool.wait_ge(adj_ready, 1)
            for l in range(1, L):
                a = adj_f[:, :, :, 0] if l == 1 else label_sum[:, :, :]
                if l > 1:
                    pool.wait_ge(pool_own, own_n)
                pool.tensor_tensor(label_sum[:, :, :], a, adj_f[:, :, :, l], ALU.add).then_inc(pool_own, 1)
                own_n += 1
            rstd_of(1, 0)
            pool.wait_ge(ld["wb"], 32)
            pool.wait_ge(pool_own, own_n)
            pool.tensor_tensor(adj_f[:, :, :, :].rearrange("p g j l -> p (g j) l"),
                               adj_f[:, :, :, :].rearrange("p g j l -> p (g j) l"),
                               wb[:, :].unsqueeze(1).broadcast_to([P, G * S, L]), ALU.mult).then_inc(pool_own, 1)
            own_n += 1
            for l in range(1, L):
                a = adj_f[:, :, :, 0] if l == 1 else label_bias[:, :, :]
                pool.wait_ge(pool_own, own_n)
                ins = pool.tensor_tensor(label_bias[:, :, :], a, adj_f[:, :, :, l], ALU.add)
                if l == L - 1:
                    ins.then_inc(labels_ready, 1)
                else:
                    ins.then_inc(pool_own, 1)
                own_n += 1
            rstd_of(1, 1)

        @block.tensor
        def _(pe):
            def turn4(ps, src):
                for i in range(4):
                    ins = pe.transpose(ps[:, i * P:(i + 1) * P], src(i), ident[:, :])
                return ins

            def dense_product(name):
                ps = psum_of(name)
                k = DENSE.index(name)
                if k >= 2:
                    pe.wait_ge(*taken(DENSE[k - 2]))
                kind, h = (name, 0) if isinstance(name, str) else name[0:2]
                bs = slice(h * BH, (h + 1) * BH)
                if kind == "small":
                    pe.wait_ge(ident_ready, 1)
                    pe.wait_ge(ld["rows"], 16 * 9)
                    return pe.transpose(ps[:, 0:ROWS], rows[0:ROWS, :], ident[0:ROWS, 0:ROWS])
                if kind == "cmod":
                    pe.wait_ge(ld["ada"], 16)
                    pe.wait_ge(silu_ready, 1)
                    for j in range(6):
                        ins = pe.matmul(ps[:, j * B:(j + 1) * B], w_ada_sb[:, j * P:(j + 1) * P], silu_c[:, :],
                                        start=True, stop=True)
                    return ins
                if kind == "xnT":
                    pe.wait_ge(xn_ready, h + 1)
                    return turn4(ps, lambda i: xn_tok[:, h * UH + i, :])
                if kind == "xT":
                    return turn4(ps, lambda i: x_tok[:, h * UH + i, :])
                if kind == "q":
                    pe.wait_ge(ld["qkv"], 16)
                    pe.wait_ge(*taken(("xnT", h)))
                    return pe.matmul(ps[:, :], w_qkv_sb[:, P:2 * P], xm[:, bs, :], start=True, stop=True)
                if kind == "k":
                    return pe.matmul(ps[:, :], w_qkv_sb[:, 0:P], xm[:, bs, :], start=True, stop=True)
                if kind == "v":
                    for u in range(UH):
                        b0 = (h * UH + u) * UB
                        ins = pe.matmul(ps[:, u * P:(u + 1) * P], xm[:, b0:b0 + UB, :], w_qkv_sb[:, 2 * P:3 * P],
                                        start=True, stop=True)
                    return ins
                if kind == "wA":
                    pe.wait_ge(ld["wrows"], 16 * 4)
                    return turn4(ps, lambda i: w_rows[:, i, :])
                if kind == "wB":
                    return turn4(ps, lambda i: w_rows[:, 4 + i, :])
                if kind == "qz":
                    pe.wait_ge(*taken("wA"))
                    return pe.matmul(ps[:, 0:B], w_cols[:, W_SELF_Q, :], cols[:, R_COND:R_COND + B], start=True, stop=True)
                if kind == "yT":
                    pe.wait_ge(y_ready, (h + 1) * UH)
                    return turn4(ps, lambda i: y_tok[:, h * UH + i, :])
                if kind == "proj":
                    pe.wait_ge(ld["proj"], 16)
                    pe.wait_ge(*taken(("yT", h)))
                    return pe.matmul(ps[:, :], w_proj_sb[:, :], yT[:, h * TH:(h + 1) * TH], start=True, stop=True)
                if kind == "x1tok":
                    pe.wait_ge(x1_ready, h + 1)
                    return turn4(ps, lambda i: x1T[:, h * BH + i * UB:h * BH + (i + 1) * UB, :])
                if kind == "xn2T":
                    pe.wait_ge(*taken(("x1tok", h)))
                    return turn4(ps, lambda i: xn_tok[:, h * UH + i, :])
                if kind == "mlp1":
                    j = name[2]
                    if j == 0:
                        pe.wait_ge(ld["mlp1"], 16)
                        pe.wait_ge(*taken(("xn2T", h)))
                    return pe.matmul(ps[:, :], w_mlp1_sb[:, j * P:(j + 1) * P], xm2[:, bs, :], start=True, stop=True)
                if kind == "mlp2":
                    pe.wait_ge(ld["mlp2"], 16)
                    for j in range(NJ):
                        pe.wait_ge(*taken(("mlp1", h, j)))
                        ins = pe.matmul(ps[:, :], w_mlp2_sb[:, j, :], hidden[:, j, :], start=(j == 0), stop=(j == NJ - 1))
                    return ins
                if kind == "rowsum":
                    pe.wait_ge(consts_ready, 1)
                    pe.wait_ge(x2_ready, h + 1)
                    return pe.matmul(ps[:, :], ones[:, :], x2T[:, bs, :], start=True, stop=True)
                if kind == "self":
                    return pe.matmul(ps[:, :], w_cols[:, W_SELF_X, :], x2T[:, bs, :], start=True, stop=True)
                if kind == "q1":
                    pe.wait_ge(*taken(("self", h)))
                    return pe.matmul(ps[:, :], w_cols[:, W_Q + name[2], :], selfT[:, bs, :], start=True, stop=True)
                if kind == "k1":
                    pe.wait_ge(*taken("wB"))
                    return pe.matmul(ps[:, 0:BH * M], w_cols[:, W_K + name[2], :], selfT[:, bs, 0:M], start=True, stop=True)
                if kind == "v1":
                    for u in range(UH):
                        b0 = (h * UH + u) * UB
                        ins = pe.matmul(ps[:, u * P:(u + 1) * P], selfT[:, b0:b0 + UB, :],
                                        w_cols[:, W_OUT + name[2], :], start=True, stop=True)
                    return ins
                if kind == "yfT":
                    pe.wait_ge(ysum_ready, h + 1)
                    return turn4(ps, lambda i: y_dir[0][:, h * UH + i, :])
                assert kind == "out"
                pe.wait_ge(outT_ready, h + 1)
                return turn4(ps, lambda i: outT[:, h * BH + i * UB:h * BH + (i + 1) * UB, :])

            for stage, i in ORDER:
                if stage == "dense":
                    dense_product(i).then_inc(dense_ready, 1)
                elif stage == "scores":
                    layer, d, g = UNITS[i]
                    h = g // UH
                    for name in ("q", "k") if layer == 0 else ("q1", "k1"):
                        pe.wait_ge(*taken((name, h) + (d,) * layer))
                    if i >= 2:
                        pe.wait_ge(*((scores_read, i - 1 - N0) if UNITS[i - 2][0] else (shifted, i - 1)))
                    nk = M if layer else S
                    for b in range(UB):
                        ins = pe.matmul(ps_s[i % 2][:, b * P:b * P + HQ * nk], Qm[d][:, g * UB + b, :, :],
                                        Kz[d][:, g * UB + b, :, 0:nk], start=True, stop=True)
                    ins.then_inc(scores_ready, 1)
                elif stage == "turn":
                    layer, d, g = UNITS[i]
                    pe.wait_ge(exp_ready, i + 1)
                    if i >= 2:
                        pe.wait_ge(pt_ready, i - 1)
                    E = E1 if layer else E0
                    for b in range(UB):
                        ins = pe.transpose(ps_t[i % 2][:, b * P:(b + 1) * P], E[:, i % 3, b * HQ:(b + 1) * HQ, :],
                                           ident[:, :])
                    ins.then_inc(turned, 1)
                elif stage == "values":
                    layer, d, g = UNITS[i]
                    pe.wait_ge(pt_ready, i + 1)
                    pe.wait_ge(*taken((("v1", g // UH, d) if layer else ("v", g // UH))))
                    if i >= 2:
                        pe.wait_ge(y_ready, i - 1)
                    for h4 in range(H4):
                        for b in range(UB):
                            ins = pe.matmul(ps_y[i % 2][QUAD * b:QUAD * b + QUAD, h4 * VW:(h4 + 1) * VW],
                                            PT[:, i % 2, b, h4 * S:(h4 + 1) * S], Vz[d][:, g * UB + b, h4, :],
                                            start=True, stop=True)
                    ins.then_inc(values_ready, 1)

        @block.scalar
        def _(act):
            act.dma_start(rows[R_COND:R_COND + B, :], cond).then_inc(ld["rows"], 16)
            for r, n, v in ((R_ADA, 6, b_ada), (R_PROJ, 1, b_proj), (R_MLP1, NJ, b_mlp1), (R_MLP2, 1, b_mlp2),
                            (R_SELF, 1, b_self)):
                act.dma_start(rows[r:r + n, :], v.rearrange("(j p) -> j p", p=P)).then_inc(ld["rows"], 16)
            for r, v in ((R_Q, bq), (R_K, bk), (R_OUT, bout)):
                act.dma_start(rows[r:r + DIRS, :], v).then_inc(ld["rows"], 16)
            act.dma_start(w_qkv_sb[:, :], w_qkv).then_inc(ld["qkv"], 16)
            act.dma_start(wb[:, :], w_bias.rearrange("(a l) -> a l", a=1).broadcast_to([P, L])).then_inc(ld["wb"], 16)
            act.dma_start(bb[:, :], b_bias.broadcast_to([P, 1])).then_inc(ld["wb"], 16)
            act.wait_ge(*taken("small"))
            act.activation(silu_t[:, 0, :], cols[:, R_COND:R_COND + B], ACT.Exp, scale=-1.0).then_inc(silu_e, 1)

            def take(name):
                ps = psum_of(name)
                act.wait_ge(dense_ready, DENSE.index(name) + 1)
                kind, h = (name, 0) if isinstance(name, str) else name[0:2]
                bs = slice(h * BH, (h + 1) * BH)
                if kind == "k":
                    act.wait_ge(kz_ready, h + 1)
                    for hq in range(HQ):
                        q = slice(QUAD * hq, QUAD * hq + QUAD)
                        ins = act.activation(Kz[0][q, bs, hq, :], ps[q, :].rearrange("p (b k) -> p b k", k=S), ACT.Copy)
                    return ins
                if kind in ("v", "v1"):
                    d = name[2] if kind == "v1" else 0
                    nk = M if kind == "v1" else S
                    if h == 0:
                        act.wait_ge(vz_ready[d], HQ)
                    for b in range(UB):
                        for hq in range(HQ):
                            src = ps[QUAD * b:QUAD * b + nk, :].rearrange("p (u q h c) -> p u q h c", u=UH, q=HQ, h=H4)
                            ins = act.activation(
                                Vz[d][QUAD * hq:QUAD * hq + nk, h * BH + b:(h + 1) * BH:UB, :, hq * C:(hq + 1) * C],
                                src[:, :, hq, :, :], ACT.Copy)
                    return ins
                if kind in ("wA", "wB"):
                    k = 0 if kind == "wA" else 4
                    return act.activation(w_cols[:, k:k + 4, :], ps[:, :].rearrange("p (j o) -> p j o", j=4), ACT.Copy)
                if kind == "qz":
                    return act.activation(qz[:, :], ps[:, 0:B], ACT.Copy)
                if kind == "xT":
                    return act.activation(xT[:, bs, :], ps[:, :].rearrange("p (b s) -> p b s", s=S), ACT.Copy)
                if kind == "yT":
                    return act.activation(yT[:, h * TH:(h + 1) * TH], ps[:, :], ACT.Copy)
                if kind == "mlp1":
                    j = name[2]
                    return act.activation(hidden[:, j, :], ps[:, :], ACT.Gelu_apprx_tanh,
                                          bias=cols[:, R_MLP1 + j:R_MLP1 + j + 1])
                if kind == "q1":
                    d = name[2]
                    for h4 in range(H4):
                        ins = act.activation(Qm[d][:, bs, h4, :], ps[:, :].rearrange("p (b q) -> p b q", q=S),
                                             ACT.Identity, scale=head_mask[:, 1, h4:h4 + 1],
                                             bias=bq_masked[:, d, h4:h4 + 1])
                    return ins
                assert kind == "out"
                return act.activation(out_tok[:, h * UH:(h + 1) * UH, :], ps[:, :].rearrange("p (u f) -> p u f", f=P),
                                      ACT.Copy)

            for stage, i in ORDER:
                if stage == "dense" and by_act(i):
                    take(i).then_inc(dense_act, 1)
                elif stage == "exp":
                    E, nk = (E1, M) if UNITS[i][0] else (E0, S)
                    act.wait_ge(shifted, i + 1)
                    act.activation(E[:, i % 3, :, 0:nk], E[:, i % 3, :, 0:nk], ACT.Exp).then_inc(exp_ready, 1)
                elif stage == "turn":
                    act.wait_ge(turned, i + 1)
                    if i >= 2:
                        act.wait_ge(values_ready, i - 1)
                    act.activation(PT[:, i % 2, :, :], ps_t[i % 2][:, :].rearrange("p (b t) -> p b t", t=P), ACT.Copy)\
                       .then_inc(pt_ready, 1)

        @block.vector
        def _(dve):
            count = [0]

            def wait_own(ins):
                count[0] += 1
                ins.then_inc(own, 1)
                dve.wait_ge(own, count[0])

            def layer_norm(layer, h, src):
                gs = slice(h * UH, (h + 1) * UH)
                for i in range(UH):
                    ins = dve.bn_stats(stats[:, h * UH + i, :], src(i))
                wait_own(ins)
                for i in range(UH):
                    ins = dve.bn_aggr(meanvar[:, h * UH + i, :], stats[:, h * UH + i, :])
                wait_own(ins)
                dve.tensor_scalar(var_eps[:, gs], meanvar[:, gs, 1], LN_EPS, None, ALU.add).then_inc(var_ready, 1)
                dve.wait_ge(rstd_ready, HALVES * layer + h + 1)
                for i in range(UH):
                    g = h * UH + i
                    ins = dve.tensor_scalar(xn_tok[:, g, :], src(i), meanvar[:, g, 0:1], rstd[:, layer, g:g + 1],
                                            ALU.subtract, ALU.mult)
                return ins

            def modulate(dst, ps, shift, scale, bs):
                wait_own(dve.tensor_tensor(dst[:, bs, :], ps[:, :].rearrange("p (b s) -> p b s", s=S),
                                           cmod[:, scale, bs].unsqueeze(2).broadcast_to([P, BH, S]), ALU.mult))
                return dve.tensor_tensor(dst[:, bs, :], dst[:, bs, :],
                                         cmod[:, shift, bs].unsqueeze(2).broadcast_to([P, BH, S]), ALU.add)

            def gated_residual(dst, ps, bias, gate, res, bs):
                ins = dve.scalar_tensor_tensor(out=gated[:, bs, :], in0=ps[:, :].rearrange("p (b s) -> p b s", s=S),
                                               scalar=cols[:, bias:bias + 1],
                                               in1=cmod[:, gate, bs].unsqueeze(2).broadcast_to([P, BH, S]),
                                               op0=ALU.add, op1=ALU.mult)
                ins.then_inc(dense_dve, 1)
                dve.wait_ge(dense_dve, dve_taken[0] + 1)
                return dve.tensor_tensor(dst[:, bs, :], gated[:, bs, :], res[:, bs, :], ALU.add)

            dve_taken = [0]

            dve.memset(Kz[0][:, 0:BH, :, :], 0.0).then_inc(kz_ready, 1)
            dve.wait_ge(ld["x0"], 16)
            layer_norm(0, 0, lambda i: x_tok[:, i, :]).then_inc(xn_ready, 1)
            dve.wait_ge(ident_ready, 1)
            wait_own(dve.tensor_reduce(head_mask[:, 0, :], ident[:, :].rearrange("p (q h c) -> p h q c", q=HQ, h=H4),
                                       AX.XY, ALU.add))
            wait_own(dve.tensor_scalar(head_mask[:, 1, :], head_mask[:, 0, :], C ** -0.5, None, ALU.mult))
            wait_own(dve.tensor_scalar(head_mask[:, 0, :], head_mask[:, 0, :], 1.0 / C, None, ALU.mult))

            def silu():
                dve.wait_ge(silu_e, 1)
                wait_own(dve.tensor_scalar(silu_t[:, 1, :], silu_t[:, 0, :], 1.0, None, ALU.add))
                wait_own(dve.reciprocal(silu_t[:, 0, :], silu_t[:, 1, :]))
                dve.tensor_tensor(silu_c[:, :], silu_t[:, 0, :], cols[:, R_COND:R_COND + B], ALU.mult)\
                   .then_inc(silu_ready, 1)
                for j in (1, 4):
                    ins = dve.tensor_scalar(cols[:, R_ADA + j:R_ADA + j + 1], cols[:, R_ADA + j:R_ADA + j + 1], 1.0,
                                            None, ALU.add)
                dve.tensor_tensor(bout_sum[:, :], cols[:, R_OUT:R_OUT + 1], cols[:, R_OUT + 1:R_OUT + 2], ALU.add)
                for d in range(DIRS):
                    ins = dve.tensor_scalar(bq_masked[:, d, :], head_mask[:, 1, :], cols[:, R_Q + d:R_Q + d + 1], None,
                                            ALU.mult)
                wait_own(ins)

            def edge_bias():
                dve.wait_ge(labels_ready, 1)
                dve.wait_ge(ld["wb"], 32)
                wait_own(dve.tensor_scalar(masked[:, :, :], label_sum[:, :, :], 0.0, NEG, ALU.is_le, ALU.mult))
                dve.scalar_tensor_tensor(out=bias_dir[:, 0, :, :], in0=label_bias[:, :, :], scalar=bb[:, 0:1],
                                         in1=masked[:, :, :], op0=ALU.add, op1=ALU.add).then_inc(bias_ready, 1)
                dve.wait_ge(bias_ready, 1)
                dve.transpose(bias_dir[:, 1, :, :], bias_dir[:, 0, :, :]).then_inc(bias_ready, 1)

            def take(name):
                ps = psum_of(name)
                dve.wait_ge(dense_ready, DENSE.index(name) + 1)
                kind, h = (name, 0) if isinstance(name, str) else name[0:2]
                bs = slice(h * BH, (h + 1) * BH)
                ps_bs = ps[:, :].rearrange("p (b s) -> p b s", s=S)
                if kind == "small":
                    dve.tensor_copy(cols[:, :], ps[:, 0:ROWS]).then_inc(dense_dve, 1)
                    dve.wait_ge(dense_dve, 1)
                    silu()
                elif kind == "cmod":
                    dve.tensor_tensor(cmod[:, :, :], ps[:, 0:6 * B].rearrange("p (j b) -> p j b", j=6),
                                      cols[:, R_ADA:R_ADA + 6].unsqueeze(2).broadcast_to([P, 6, B]), ALU.add)\
                       .then_inc(dense_dve, 1)
                    dve.wait_ge(dense_dve, 2)
                elif kind == "xnT":
                    modulate(xm, ps, 0, 1, bs).then_inc(dense_dve, 1)
                    if h == 0:
                        dve.wait_ge(ld["x1"], 16)
                        dve.memset(Kz[0][:, BH:B, :, :], 0.0).then_inc(kz_ready, 1)
                        layer_norm(0, 1, lambda i: x_tok[:, UH + i, :]).then_inc(xn_ready, 1)
                elif kind == "q":
                    for h4 in range(H4):
                        ins = dve.tensor_scalar(Qm[0][:, bs, h4, :], ps_bs, head_mask[:, 0, h4:h4 + 1], None, ALU.mult)
                    ins.then_inc(dense_dve, 1)
                elif kind == "proj":
                    if h == 0:
                        dve.wait_ge(*taken(("xT", 1)))
                    gated_residual(x1T, ps, R_PROJ, 2, xT, bs).then_inc(x1_ready, 1)
                elif kind == "x1tok":
                    layer_norm(1, h, lambda i: ps[:, i * P:(i + 1) * P]).then_inc(dense_dve, 1)
                elif kind == "xn2T":
                    modulate(xm2, ps, 3, 4, bs).then_inc(dense_dve, 1)
                elif kind == "mlp2":
                    dve.wait_ge(x1_ready, h + 1)
                    gated_residual(x2T, ps, R_MLP2, 5, x1T, bs).then_inc(x2_ready, 1)
                elif kind == "rowsum":
                    dve.wait_ge(*taken("qz"))
                    dve.scalar_tensor_tensor(out=zeroed_q[:, :, :], in0=ps_bs, scalar=0.0,
                                             in1=qz[:, bs].unsqueeze(2).broadcast_to([P, BH, S]),
                                             op0=ALU.not_equal, op1=ALU.mult).then_inc(dense_dve, 1)
                    dve.wait_ge(dense_dve, dve_taken[0] + 1)
                elif kind == "self":
                    dve.scalar_tensor_tensor(out=selfT[:, bs, :], in0=ps_bs, scalar=cols[:, R_SELF:R_SELF + 1],
                                             in1=zeroed_q[:, :, :], op0=ALU.add, op1=ALU.add).then_inc(dense_dve, 1)
                elif kind == "q1":
                    d = name[2]
                    for h4 in range(H4):
                        ins = dve.tensor_scalar(Qm[d][:, bs, h4, :], ps_bs, cols[:, R_Q + d:R_Q + d + 1],
                                                head_mask[:, 1, h4:h4 + 1], ALU.add, ALU.mult)
                    ins.then_inc(dense_dve, 1)
                elif kind == "k1":
                    d = name[2]
                    if d == 1 and h == 0:
                        dve.wait_ge(kz1_ready, 1)
                    for hq in range(HQ):
                        q = slice(QUAD * hq, QUAD * hq + QUAD)
                        ins = dve.tensor_scalar(Kz[d][q, bs, hq, 0:M],
                                                ps[q, 0:BH * M].rearrange("p (b k) -> p b k", k=M),
                                                cols[q, R_K + d:R_K + d + 1], None, ALU.add)
                    ins.then_inc(dense_dve, 1)
                else:
                    assert kind == "yfT"
                    dve.scalar_tensor_tensor(out=rT[:, bs, :], in0=ps_bs, scalar=bout_sum[:, 0:1], in1=selfT[:, bs, :],
                                             op0=ALU.add, op1=ALU.add).then_inc(dense_dve, 1)
                    dve.wait_ge(dense_dve, dve_taken[0] + 1)
                    dve.scalar_tensor_tensor(out=outT[:, bs, :], in0=rT[:, bs, :], scalar=0.0, in1=x2T[:, bs, :],
                                             op0=ALU.max, op1=ALU.add).then_inc(outT_ready, 1)
                dve_taken[0] += 1

            for stage, i in ORDER:
                if stage == "dense" and not by_act(i):
                    take(i)
                elif stage == "shift":
                    layer, d, g = UNITS[i]
                    dve.wait_ge(scores_ready, i + 1)
                    if i >= 3:
                        dve.wait_ge(turned, i - 2)
                    if i == 1:
                        dve.wait_ge(ld["adj"], 16)
                        dve.tensor_copy(adj_f[:, :, :, :].rearrange("p g j l -> p g (j l)"), adj_i[:, :, :])\
                           .then_inc(adj_ready, 1)
                    if i == N0:
                        dve.memset(E1[:, :, :, M:S], 0.0)
                        edge_bias()
                    nm = neg_max[:, i % 2, :]
                    sc = ps_s[i % 2][:, :].rearrange("p (j k) -> p j k", k=S)
                    e = E0[:, i % 3, :, :]
                    if layer:
                        if g % UH == 0:
                            dve.wait_ge(bias_spread[d], 16 * UB * H4)
                        e = E1[:, i % 3, :, 0:M]
                        dve.tensor_tensor(e.rearrange("p (b q) k -> p b q k", b=UB),
                                          ps_s[i % 2][:, :].rearrange("p (b r) -> p b r", b=UB)[:, :, 0:HQ * M]
                                          .rearrange("p b (q k) -> p b q k", k=M),
                                          bias_rep[d][:, g * UB:(g + 1) * UB, :].unsqueeze(2)
                                          .broadcast_to([P, UB, HQ, M]), ALU.add).then_inc(scores_read, 1)
                        dve.wait_ge(scores_read, i + 1 - N0)
                        sc = e
                    wait_own(dve.tensor_reduce(nm, sc, AX.X, ALU.max, negate=True))
                    dve.tensor_tensor(e, sc, nm.unsqueeze(2).broadcast_to([P, UB * HQ, sc.shape[2]]), ALU.add)\
                       .then_inc(shifted, 1)
                elif stage == "normalise":
                    layer, d, g = UNITS[i]
                    dve.wait_ge(values_ready, i + 1)
                    yv = ps_y[i % 2][:, 0:H4 * VW].rearrange("p (h w) -> p h w", w=VW)
                    wait_own(dve.reciprocal(rden[:, i % 2, :, :], yv[:, :, HQ * C:VW]))
                    dst = (y_dir[d][:, g, :] if layer else y_tok[:, g, :]).rearrange("p (q h c) -> p h q c", q=HQ, h=H4)
                    dve.tensor_tensor(dst, yv[:, :, 0:HQ * C].rearrange("p h (q c) -> p h q c", c=C),
                                      rden[:, i % 2, :, :].unsqueeze(3).broadcast_to([P, H4, HQ, C]), ALU.mult)\
                       .then_inc(y_ready, 1)
                    if layer and d == 1 and g % UH == UH - 1:
                        h = g // UH
                        dve.wait_ge(y_ready, i + 1)
                        dve.tensor_tensor(y_dir[0][:, h * UH:(h + 1) * UH, :], y_dir[0][:, h * UH:(h + 1) * UH, :],
                                          y_dir[1][:, h * UH:(h + 1) * UH, :], ALU.add).then_inc(ysum_ready, 1)


_INS = ["x", "cond_1024", "mask_BxSxSx11_ik0", "L0_cond_w_ada", "L0_cond_b_ada", "L0_cond_w_qkv", "L0_cond_w_proj",
        "L0_cond_b_proj", "L0_cond_w_mlp1", "L0_cond_b_mlp1", "L0_cond_w_mlp2", "L0_cond_b_mlp2", "L1_cond_W_self",
        "L1_cond_b_self", "L1_cond_w_bias", "L1_cond_b_bias", "L1_cond_Wq", "L1_cond_bq", "L1_cond_Wk", "L1_cond_bk",
        "L1_cond_Wout", "L1_cond_bout"]


def kernel(**inputs):
    import numpy as np
    import concourse.bacc as bacc
    from concourse.bass_utils import run_bass_kernel_spmd

    nc = bacc.Bacc("TRN2", target_bir_lowering=False, num_devices=1)
    arrays, args = {}, []
    for name in _INS:
        a = np.ascontiguousarray(inputs[name])
        if a.ndim == 0:
            a = a.reshape(1, 1)
        arrays[f"in_{name}"] = a
        args.append(nc.dram_tensor(f"in_{name}", a.shape, mybir.dt.from_np(a.dtype), kind="ExternalInput").ap())
    args.append(nc.dram_tensor("out_0", (B, S, P), F32, kind="ExternalOutput").ap())
    program(nc, *args)
    r = run_bass_kernel_spmd(nc, [arrays], core_ids=[0])
    return r.results[0]["out_0"]
```

```python
from contextlib import ExitStack

import concourse.bass as bass
from concourse import mybir

ALU = mybir.AluOpType
ACT = mybir.ActivationFunctionType
F32 = mybir.dt.float32
I32 = mybir.dt.int32
AX = mybir.AxisListType

P = 128
B = 32
S = 32
QUAD = 32
HQ = 4
H4 = 4
C = 8
G = 8
UB = 4
HALVES = 2
BH = B // HALVES
UH = G // HALVES
TH = BH * S
M = 20
L = 11
NJ = 4
VW = HQ * C + HQ
LN_EPS = 1e-6
NEG = -9000000000000000.0
DIRS = 2

R_COND = 0
R_ADA = B
R_PROJ = R_ADA + 6
R_MLP1 = R_PROJ + 1
R_MLP2 = R_MLP1 + NJ
R_SELF = R_MLP2 + 1
R_Q = R_SELF + 1
R_K = R_Q + DIRS
R_OUT = R_K + DIRS
R_LABEL = R_OUT + DIRS
COLS = R_LABEL + L + 1

UNITS = [(0, 0, g) for g in range(G)]
for _h in range(HALVES):
    for _d in range(DIRS):
        UNITS += [(1, _d, _h * UH + _u) for _u in range(UH)]
N0 = G
SUB_POOL = True


ENDS = [(0, 4), (4, 7), (7, 8)]

PARTS = {"q": 4, "q1": 4, "k": 2, "k1": 2, "v": 4, "v1": 4, "x1tok": 2}


POOL_Q = []


def kind_of(name):
    return name if isinstance(name, str) else name[0]


def parts_of(name):
    return 1 if name in POOL_Q else PARTS.get(kind_of(name), 1)


def take(name, *parts):
    masks = [("mask", (name, h4)) for h4 in range(H4)] if name in POOL_Q else []
    return [("take", (name, p)) for p in (parts or range(parts_of(name))) if p < parts_of(name)] + masks * (0 in (parts or (0,)))


def make(*names):
    return [("dense", n) for n in names]


def dense(*names):
    return [t for n in names for t in make(n) + take(n)]


def attention(first, count, fill, late={}):
    order = []
    last = first + count
    for s in range(first - 2, last):
        if first <= s + 1 < last:
            order += [("exp", s + 1)]
        if s + 2 < last:
            order += [("scores", s + 2), ("soft", (s + 2, s - 1 if s - 1 >= first else None))]
            order += [("sub", s + 2)] * (s + 2 >= N0 and SUB_POOL)
        elif s - 1 >= first:
            order += [("soft", (None, s - 1))]
        if first <= s + 1 < last:
            order += [("turn", s + 1), ("copy", s + 1)]
        order += fill.get(s - first, [])
        if s >= first:
            order += [("values", s)]
        order += late.get(s - first, [])
    return order + [("soft", (None, last - 1))]


ORDER = [
    ("dense", ("cmod", 0)), ("dense", ("xnT", 0)), ("take", (("cmod", 0), 0)), ("take", (("xnT", 0), 0)),
    ("dense", ("q", 0)), ("dense", ("k", 0)), ("norm1", 0), ("take", (("q", 0), 0)), ("take", (("q", 0), 3)),
    ("take", (("q", 0), 1)), ("take", (("k", 0), 1)), ("take", (("q", 0), 2)), ("norm1", 1),
    ("take", (("k", 0), 0)), ("dense", ("v", 0)),
    ("scores", 0), ("soft", (0, None)), ("exp", 0),
    ("scores", 1), ("dense", ("xnT", 1)), ("soft", (1, None)), ("take", (("xnT", 1), 0)), ("turn", 0),
    ("scores", 2), ("take", (("v", 0), 0)), ("take", (("v", 0), 1)), ("take", (("v", 0), 3)),
    ("take", (("v", 0), 2)), ("exp", 1), ("copy", 0), ("turn", 1), ("dense", ("q", 1)), ("copy", 1),
    ("take", (("q", 1), 0)),
    ("scores", 3), ("dense", ("k", 1)), ("take", (("q", 1), 3)), ("soft", (2, None)), ("exp", 2),
    ("take", (("k", 1), 0)), ("values", 0), ("dense", "qz"), ("soft", (3, 0)), ("turn", 2), ("values", 1),
    ("take", ("qz", 0)), ("take", (("q", 1), 1)), ("take", (("q", 1), 2)), ("dense", ("v", 1)),
    ("take", (("k", 1), 1)),
    ("scores", 4), ("soft", (4, 1)), ("copy", 2),
    ("scores", 5), ("dense", ("cmod", 1)), ("values", 2), ("take", (("cmod", 1), 0)), ("soft", (5, 2)),
    ("take", (("v", 1), 0)), ("take", (("v", 1), 3)), ("take", (("v", 1), 2)), ("exp", 3), ("turn", 3),
    ("scores", 6), ("exp", 4), ("copy", 3), ("take", (("v", 1), 1)), ("values", 3), ("turn", 4), ("exp", 5),
    ("copy", 4), ("soft", (6, 3)), ("turn", 5), ("values", 4), ("dense", ("yT", 0)), ("take", (("yT", 0), 0)),
    ("exp", 6), ("copy", 5), ("dense", ("proj", 0)), ("turn", 6), ("take", (("proj", 0), 0)),
    ("dense", ("x1tok", 0)),
    ("scores", 7), ("values", 5), ("copy", 6), ("take", (("x1tok", 0), 0)), ("soft", (7, 4)), ("exp", 7),
    ("turn", 7), ("copy", 7), ("take", (("x1tok", 0), 1)), ("soft", (None, 5)), ("dense", ("xn2T", 0)),
    ("values", 6), ("take", (("xn2T", 0), 0)), ("soft", (None, 6)), ("values", 7), ("dense", ("mlp1", 0, 1)),
    ("dense", ("mlp1", 0, 0)), ("soft", (None, 7)), ("edges", 0), ("dense", ("yT", 1)),
    ("take", (("mlp1", 0, 1), 0)), ("take", (("mlp1", 0, 0), 0)), ("take", (("yT", 1), 0)),
    ("dense", ("mlp1", 0, 2)), ("dense", ("proj", 1)), ("take", (("mlp1", 0, 2), 0)), ("take", (("proj", 1), 0)),
    ("dense", ("mlp1", 0, 3)), ("dense", ("x1tok", 1)), ("take", (("mlp1", 0, 3), 0)), ("take", (("x1tok", 1), 0)),
    ("dense", ("mlp2", 0)), ("take", (("x1tok", 1), 1)), ("dense", ("xn2T", 1)), ("take", (("mlp2", 0), 0)),
    ("take", (("xn2T", 1), 0)), ("dense", ("rowsum", 0)), ("dense", ("self", 0)), ("take", (("rowsum", 0), 0)),
    ("take", (("self", 0), 0)), ("dense", ("mlp1", 1, 1)), ("dense", ("q1", 0, 0)), ("dense", ("mlp1", 1, 2)),
    ("take", (("mlp1", 1, 1), 0)), ("take", (("q1", 0, 0), 1)), ("take", (("q1", 0, 0), 0)),
    ("take", (("q1", 0, 0), 2)), ("take", (("q1", 0, 0), 3)), ("take", (("mlp1", 1, 2), 0)),
    ("dense", ("mlp1", 1, 0)), ("take", (("mlp1", 1, 0), 0)), ("dense", ("k1", 0, 0)), ("take", (("k1", 0, 0), 1)),
    ("take", (("k1", 0, 0), 0)), ("dense", ("v1", 0, 0)), ("dense", ("mlp1", 1, 3)),
    ("scores", 8), ("soft", (8, None)), ("sub", 8),
    ("scores", 9), ("soft", (9, None)), ("sub", 9), ("take", (("v1", 0, 0), 3)), ("take", (("v1", 0, 0), 0)),
    ("take", (("mlp1", 1, 3), 0)), ("dense", ("mlp2", 1)), ("exp", 8), ("take", (("v1", 0, 0), 1)), ("exp", 9),
    ("take", (("v1", 0, 0), 2)), ("dense", ("q1", 0, 1)), ("turn", 8), ("copy", 8),
    ("scores", 10), ("turn", 9),
    ("scores", 11), ("values", 8), ("take", (("q1", 0, 1), 1)), ("take", (("mlp2", 1), 0)), ("soft", (10, None)),
    ("take", (("q1", 0, 1), 3)), ("copy", 9), ("sub", 10), ("take", (("q1", 0, 1), 2)), ("dense", ("k1", 0, 1)),
    ("values", 9), ("soft", (11, 8)), ("sub", 11), ("take", (("k1", 0, 1), 1)), ("take", (("k1", 0, 1), 0)),
    ("take", (("q1", 0, 1), 0)), ("exp", 10), ("turn", 10), ("dense", ("v1", 0, 1)), ("copy", 10), ("exp", 11),
    ("values", 10), ("turn", 11),
    ("scores", 12), ("soft", (12, 9)), ("sub", 12),
    ("scores", 13), ("take", (("v1", 0, 1), 0)), ("take", (("v1", 0, 1), 3)), ("copy", 11),
    ("take", (("v1", 0, 1), 1)), ("exp", 12), ("take", (("v1", 0, 1), 2)), ("soft", (13, 10)), ("sub", 13),
    ("dense", ("rowsum", 1)), ("dense", ("self", 1)), ("take", (("rowsum", 1), 0)), ("take", (("self", 1), 0)),
    ("scores", 14), ("turn", 12), ("dense", ("q1", 1, 0)), ("copy", 12), ("exp", 13), ("take", (("q1", 1, 0), 3)),
    ("dense", ("k1", 1, 0)), ("dense", ("v1", 1, 0)), ("values", 11), ("soft", (14, 11)), ("sub", 14), ("turn", 13),
    ("scores", 15), ("values", 12), ("soft", (15, 12)), ("sub", 15), ("take", (("q1", 1, 0), 0)),
    ("take", (("q1", 1, 0), 2)), ("take", (("q1", 1, 0), 1)), ("dense", ("q1", 1, 1)), ("copy", 13),
    ("take", (("k1", 1, 0), 0)), ("exp", 14), ("take", (("k1", 1, 0), 1)), ("turn", 14), ("values", 13),
    ("scores", 16), ("copy", 14),
    ("scores", 17), ("values", 14), ("take", (("q1", 1, 1), 2)), ("take", (("v1", 1, 0), 1)), ("exp", 15),
    ("turn", 15), ("dense", ("k1", 1, 1)), ("take", (("v1", 1, 0), 0)), ("take", (("q1", 1, 1), 0)),
    ("soft", (16, 13)), ("sub", 16), ("soft", (17, 14)), ("sub", 17),
    ("scores", 18), ("copy", 15), ("exp", 16), ("turn", 16), ("values", 15),
    ("scores", 19), ("take", (("v1", 1, 0), 3)), ("exp", 17), ("copy", 16), ("turn", 17),
    ("take", (("v1", 1, 0), 2)), ("take", (("q1", 1, 1), 3)), ("values", 16), ("copy", 17),
    ("take", (("k1", 1, 1), 0)), ("soft", (18, 15)), ("sub", 18), ("soft", (19, 16)), ("sub", 19),
    ("take", (("q1", 1, 1), 1)), ("dense", ("v1", 1, 1)), ("values", 17), ("take", (("k1", 1, 1), 1)), ("exp", 18),
    ("turn", 18), ("dense", ("yfT", 0)),
    ("scores", 20), ("take", (("yfT", 0), 0)), ("soft", (20, 17)), ("sub", 20), ("take", (("v1", 1, 1), 3)),
    ("exp", 19), ("copy", 18), ("values", 18), ("turn", 19), ("take", (("v1", 1, 1), 0)),
    ("take", (("v1", 1, 1), 2)), ("copy", 19), ("exp", 20), ("take", (("v1", 1, 1), 1)),
    ("scores", 21), ("dense", ("out", 0)), ("soft", (21, 18)), ("sub", 21),
    ("scores", 22), ("turn", 20), ("values", 19), ("soft", (22, 19)), ("sub", 22), ("copy", 20), ("exp", 21),
    ("values", 20), ("turn", 21), ("copy", 21), ("exp", 22),
    ("scores", 23), ("soft", (23, 20)), ("sub", 23), ("turn", 22), ("values", 21), ("soft", (None, 21)),
    ("copy", 22), ("exp", 23), ("values", 22), ("turn", 23), ("take", (("out", 0), 0)), ("copy", 23),
    ("soft", (None, 22)), ("values", 23), ("dense", ("yfT", 1)), ("soft", (None, 23)), ("take", (("yfT", 1), 0)),
    ("dense", ("yfT", 2)), ("dense", ("out", 1)), ("take", (("out", 1), 0)), ("take", (("yfT", 2), 0)),
    ("dense", ("out", 2)), ("take", (("out", 2), 0)),
]
DENSE = [i for stage, i in ORDER if stage == "dense"]
TAKES = [i for stage, i in ORDER if stage == "take"]

ACT_PARTS = {"k": (0, 1), "v": (0, 1, 2, 3), "k1": (0, 1), "v1": (0, 1, 2, 3), "qz": (0,), "yT": (0,), "mlp1": (0,),
             "out": (0,), ("q1", 0, 0): (0, 1, 2, 3), ("q", 1): (0, 1, 2, 3), ("q1", 1, 1): (), ("k1", 0, 1): (),
             ("k", 1): (1,), ("q", 0): (0, 1, 2, 3), ("q1", 0, 1): (0, 1, 2, 3), ("k1", 1, 1): (1,),
             ("k1", 1, 0): (0, 1), ("k", 0): (1,), ("q1", 1, 0): (0, 1, 2, 3), ("k1", 0, 0): (1,)}
ADA_CHUNKS = [(0, 2), (2, 6)]


def by_act(name, part):
    if name in POOL_Q:
        return True
    return part in ACT_PARTS.get(name, ACT_PARTS.get(kind_of(name), ()))


def last_takes(act):
    names = [name for name, part in TAKES if by_act(name, part) == act]
    return [n for i, n in enumerate(names) if n not in names[i + 1:]]


def is_last_part(name, part):
    parts = [p for n, p in TAKES if n == name and by_act(n, p) == by_act(name, part)]
    return parts[-1] == part


def program(nc, cols, x_tok, xT, adj, w_ada, w_qkv, w_rest, out):
    x_dram, xT_dram, cols_dram, adj_dram = x_tok, xT, cols, adj
    with ExitStack() as ctx:
        def sb(name, shape, dt=F32):
            return ctx.enter_context(nc.sbuf_tensor(name, shape, dt))

        def sem(name):
            return ctx.enter_context(nc.semaphore(name))

        ident = sb("ident", [P, P])
        ones = sb("ones", [P, P])
        head_mask = sb("head_mask", [P, 3, H4])
        minus_half = sb("minus_half", [P, UH])
        cols = sb("cols", [P, COLS])
        wb = cols[:, R_LABEL:R_LABEL + L]
        bb = cols[:, R_LABEL + L:COLS]
        silu_t = sb("silu_t", [P, 2, B])
        silu_c = sb("silu_c", [P, B])
        cmod = sb("cmod", [P, 6, B])
        bout_sum = sb("bout_sum", [P, 1])
        bq_masked = sb("bq_masked", [P, DIRS, H4])
        qz = sb("qz", [P, B])
        x_tok = sb("x_tok", [P, G, P])
        xn_tok = sb("xn_tok", [P, G, P])
        stats = sb("stats", [P, G, 6])
        meanvar = sb("meanvar", [P, G, 2])
        var_eps = sb("var_eps", [P, G])
        rstd = sb("rstd", [P, 2, G])
        xT = sb("xT", [P, B, S])
        xm = sb("xm", [P, B, S])
        xm2 = xm
        gated = sb("gated", [P, B, S])
        x1T = sb("x1T", [P, B, S])
        x2T = sb("x2T", [P, B, S])
        zeroed_q = sb("zeroed_q", [P, BH, S])
        selfT = sb("selfT", [P, B, S])
        hidden = sb("hidden", [P, NJ, TH])
        y_tok = sb("y_tok", [P, G, P])
        yT = sb("yT", [P, B * S])
        y_dir = [yT[:, :].rearrange("p (g f) -> p g f", f=P), y_tok[:, :, :]]
        Qm = [sb(f"Qm{d}", [P, B, H4, S]) for d in range(DIRS)]
        Kz = [sb(f"Kz{d}", [P, B, HQ, S]) for d in range(DIRS)]
        Vz = [sb(f"Vz{d}", [P, B, H4, VW]) for d in range(DIRS)]
        E0 = sb("E0", [P, 3, UB * HQ, S])
        E1 = sb("E1", [P, 3, UB * HQ, S])
        q_flat = sb("q_flat", [P, 2, BH, S])
        PT = sb("PT", [P, 2, UB, P])
        neg_max = sb("neg_max", [P, 3, UB * HQ])
        rden = sb("rden", [P, 2, H4, HQ])
        w_ada_sb = sb("w_ada_sb", [P, 6 * P])
        w_qkv_sb = sb("w_qkv_sb", [P, 3 * P])
        w_rest_sb = sb("w_rest_sb", [P, 17, P])
        w_proj_sb = w_rest_sb[:, 0, :]
        w_mlp1_sb = w_rest_sb[:, 1:1 + NJ, :]
        w_mlp2_sb = w_rest_sb[:, 5:5 + NJ, :]
        w_cols = w_rest_sb[:, 9:17, :]
        adj_i = Qm[1][:, :, :, :].rearrange("p b h s -> p (b h s)")[:, 0:G * S * L].bitcast(I32)\
            .rearrange("p (g r) -> p g r", g=G)
        adj_f = sb("adj_f", [P, G, S, L])
        label_sum = sb("label_sum", [P, G, S])
        label_bias = sb("label_bias", [P, G, S])
        masked = sb("masked", [P, G, S])
        bias_dir = sb("bias_dir", [P, DIRS, G, S])
        bias_rep = sb("bias_rep", [P, DIRS, B, M])
        bias_dram = nc.dram_tensor("bias_dram", (S, DIRS, B, M), F32, kind="Internal").ap()
        out_tok = x_tok
        outT = x1T
        rT = gated
        W_SELF_X, W_SELF_Q, W_Q, W_K, W_OUT = 0, 1, 2, 4, 6

        def bank(name):
            return ctx.enter_context(nc.psum_tensor(name, [P, 512], F32))
        ps_s = [bank(f"ps_s{i}") for i in range(2)]
        ps_t = bank("ps_t")
        ps_y = [bank(f"ps_y{i}") for i in range(2)]
        ps_d = [bank(f"ps_d{i}") for i in range(3)]

        ld = {n: sem("ld_" + n) for n in ("cols", "x0", "x1", "ada", "qkv", "xT", "adj", "rest")}
        stored = sem("stored")
        ident_ready = sem("ident_ready")
        consts_ready = sem("consts_ready")
        kz_ready = sem("kz_ready")
        kz1_ready = sem("kz1_ready")
        vz_ready = [sem(f"vz_ready{d}") for d in range(DIRS)]
        dense_ready = sem("dense_ready")
        dense_act = sem("dense_act")
        dense_dve = sem("dense_dve")
        scores_ready = sem("scores_ready")
        scores_read = sem("scores_read")
        shifted = sem("shifted")
        exp_ready = sem("exp_ready")
        max_ready = sem("max_ready")
        rden_ready = sem("rden_ready")
        q_masked = sem("q_masked")
        masks_ready = sem("masks_ready")
        turned = sem("turned")
        pt_ready = sem("pt_ready")
        values_ready = sem("values_ready")
        y_ready = sem("y_ready")
        own = sem("own")
        var_ready = sem("var_ready")
        rstd_ready = sem("rstd_ready")
        xn_ready = sem("xn_ready")
        x1_ready = sem("x1_ready")
        x2_ready = sem("x2_ready")
        silu_e = sem("silu_e")
        silu_ready = sem("silu_ready")
        ysum_ready = sem("ysum_ready")
        outT_ready = sem("outT_ready")
        adj_ready = sem("adj_ready")
        labels_ready = sem("labels_ready")
        pool_own = sem("pool_own")
        bias_ready = sem("bias_ready")
        bias_out = sem("bias_out")
        bias_spread = sem("bias_spread")

        def wait_taken(engine, name):
            for sem_taken, act in ((dense_act, True), (dense_dve, False)):
                names = last_takes(act)
                if name in names:
                    engine.wait_ge(sem_taken, names.index(name) + 1)

        def psum_of(name):
            return ps_d[DENSE.index(name) % len(ps_d)]

        block = ctx.enter_context(nc.Block())

        @block.sync
        def _(sp):
            sp.dma_start(cols[:, :], cols_dram).then_inc(ld["cols"], 16)
            sp.dma_start(w_ada_sb[:, :], w_ada).then_inc(ld["ada"], 16)
            sp.dma_start(w_qkv_sb[:, :], w_qkv).then_inc(ld["qkv"], 16)
            sp.dma_start(adj_i[:, :, :], adj_dram).then_inc(ld["adj"], 16)
            sp.dma_start(w_rest_sb[:, :, :], w_rest.rearrange("p (j o) -> p j o", o=P)).then_inc(ld["rest"], 16)
            sp.wait_ge(bias_ready, 2)
            for b in range(UB):
                sp.dma_start(bias_dram[:, :, b:B:UB, :], bias_dir[QUAD * b:QUAD * b + QUAD, :, :, 0:M])\
                  .then_inc(bias_out, 16)
            sp.wait_ge(bias_out, 16 * UB)
            for h4 in range(H4):
                sp.dma_start(bias_rep[QUAD * h4:QUAD * h4 + QUAD, :, :, :], bias_dram).then_inc(bias_spread, 16)
            o_v = out.rearrange("(g b) s f -> (b s) g f", b=UB)
            for e, (g0, g1) in enumerate(ENDS):
                wait_taken(sp, ("out", e))
                sp.dma_start(o_v[:, g0:g1, :], out_tok[:, g0:g1, :]).then_inc(stored, 16)
            sp.wait_ge(stored, 16 * len(ENDS))

        @block.gpsimd
        def _(pool):
            pool.memset(ident[:, :], 0.0).then_inc(pool_own, 1)
            pool.wait_ge(pool_own, 1)
            pool.affine_select(out=ident[:, :], in_=ident[:, :], compare_op=ALU.not_equal, fill=1.0, base=0,
                               pattern=[[-1, P]], channel_multiplier=1).then_inc(ident_ready, 1)
            pool.memset(minus_half[:, :], -0.5).then_inc(pool_own, 1)

            def ones_block(d, bs):
                for hq in range(HQ):
                    pool.memset(Vz[d][QUAD * hq:QUAD * hq + QUAD, bs, :, HQ * C + hq], 1.0).then_inc(vz_ready[d], 1)

            def rstd_of(layer, h):
                pool.wait_ge(var_ready, HALVES * layer + h + 1)
                pool.tensor_tensor(rstd[:, layer, h * UH:(h + 1) * UH], var_eps[:, h * UH:(h + 1) * UH],
                                   minus_half[:, :], ALU.pow).then_inc(rstd_ready, 1)

            pool.memset(Vz[0][:, 0:BH, :, :], 0.0).then_inc(pool_own, 1)
            pool.wait_ge(pool_own, 3)
            rstd_of(0, 0)
            pool.wait_ge(rstd_ready, 1)
            ones_block(0, slice(0, BH))
            pool.wait_ge(vz_ready[0], HQ)
            pool.memset(Kz[0][:, BH:B, :, :], 0.0).then_inc(kz_ready, 1)
            rstd_of(0, 1)
            pool.memset(Vz[0][:, BH:B, :, :], 0.0).then_inc(pool_own, 1)
            pool.wait_ge(pool_own, 4)
            pool.wait_ge(rstd_ready, 2)
            ones_block(0, slice(BH, B))
            pool.wait_ge(vz_ready[0], HALVES * HQ)
            pool.memset(E1[:, :, :, M:S], 0.0)
            pool.memset(ones[:, :], 1.0).then_inc(consts_ready, 1)
            own_n = 4
            pool.wait_ge(adj_ready, 1)
            for l in range(1, L):
                a = adj_f[:, :, :, 0] if l == 1 else label_sum[:, :, :]
                if l > 1:
                    pool.wait_ge(pool_own, own_n)
                pool.tensor_tensor(label_sum[:, :, :], a, adj_f[:, :, :, l], ALU.add).then_inc(pool_own, 1)
                own_n += 1
            pool.wait_ge(ld["cols"], 16)
            pool.wait_ge(pool_own, own_n)
            for g in range(0, G, 2):
                flat = adj_f[:, g:g + 2, :, :].rearrange("p g j l -> p (g j) l")
                pool.tensor_tensor(flat, flat, wb.unsqueeze(1).broadcast_to([P, 2 * S, L]), ALU.mult).then_inc(pool_own, 1)
                own_n += 1
            for l in range(1, L):
                a = adj_f[:, :, :, 0] if l == 1 else label_bias[:, :, :]
                pool.wait_ge(pool_own, own_n)
                ins = pool.tensor_tensor(label_bias[:, :, :], a, adj_f[:, :, :, l], ALU.add)
                if l == L - 1:
                    ins.then_inc(labels_ready, 1)
                else:
                    ins.then_inc(pool_own, 1)
                own_n += l < L - 1
            rstd_of(1, 0)
            pool.memset(Kz[1][:, :, :, :], 0.0).then_inc(kz1_ready, 1)
            pool.memset(Vz[1][:, :, :, :], 0.0).then_inc(pool_own, 1)
            own_n += 1
            pool.wait_ge(pool_own, own_n)
            ones_block(1, slice(0, B))
            pool.wait_ge(vz_ready[1], HQ)

            rstd_of(1, 1)
            for stage, i in ORDER:
                if stage == "sub":
                    pool.wait_ge(max_ready, i + 1)
                    e, nm = E1[:, i % 3, :, 0:M], neg_max[:, i % 3, :]
                    pool.tensor_tensor(e, e, nm.unsqueeze(2).broadcast_to([P, UB * HQ, M]), ALU.add).then_inc(shifted, 1)
                elif stage == "mask":
                    (_, h, d), h4 = i
                    wait_taken(pool, i[0])
                    pool.wait_ge(masks_ready, 1)
                    pool.tensor_tensor(Qm[d][:, h * BH:(h + 1) * BH, h4, :], q_flat[:, POOL_Q.index(i[0]) % 2, :, :],
                                       head_mask[:, 1, h4:h4 + 1].unsqueeze(2).broadcast_to([P, BH, S]), ALU.mult)\
                        .then_inc(q_masked, 1)

        @block.tensor
        def _(pe):
            def turn4(ps, src, count=4):
                for i in range(count):
                    ins = pe.transpose(ps[:, i * P:(i + 1) * P], src(i), ident[:, :])
                return ins

            def dense_product(name):
                ps = psum_of(name)
                k = DENSE.index(name)
                if k >= len(ps_d):
                    wait_taken(pe, DENSE[k - len(ps_d)])
                kind, h = (name, 0) if isinstance(name, str) else name[0:2]
                bs = slice(h * BH, (h + 1) * BH)
                if kind == "cmod":
                    pe.wait_ge(ld["ada"], 16)
                    pe.wait_ge(silu_ready, 1)
                    for j in range(*ADA_CHUNKS[h]):
                        ins = pe.matmul(ps[:, j * B:(j + 1) * B], w_ada_sb[:, j * P:(j + 1) * P], silu_c[:, :],
                                        start=True, stop=True)
                    return ins
                if kind == "xnT":
                    if h == 0:
                        pe.wait_ge(ident_ready, 1)
                    pe.wait_ge(xn_ready, h + 1)
                    return turn4(ps, lambda i: xn_tok[:, h * UH + i, :])
                if kind == "q":
                    pe.wait_ge(ld["qkv"], 16)
                    wait_taken(pe, ("xnT", h))
                    return pe.matmul(ps[:, :], w_qkv_sb[:, P:2 * P], xm[:, bs, :], start=True, stop=True)
                if kind == "k":
                    return pe.matmul(ps[:, :], w_qkv_sb[:, 0:P], xm[:, bs, :], start=True, stop=True)
                if kind == "v":
                    for u in range(UH):
                        b0 = (h * UH + u) * UB
                        ins = pe.matmul(ps[:, u * P:(u + 1) * P], xm[:, b0:b0 + UB, :], w_qkv_sb[:, 2 * P:3 * P],
                                        start=True, stop=True)
                    return ins
                if kind == "qz":
                    pe.wait_ge(ld["rest"], 16)
                    return pe.matmul(ps[:, 0:B], w_cols[:, W_SELF_Q, :], cols[:, R_COND:R_COND + B], start=True, stop=True)
                if kind == "yT":
                    pe.wait_ge(y_ready, (h + 1) * UH)
                    return turn4(ps, lambda i: y_tok[:, h * UH + i, :])
                if kind == "proj":
                    pe.wait_ge(ld["rest"], 16)
                    wait_taken(pe, ("yT", h))
                    return pe.matmul(ps[:, :], w_proj_sb, yT[:, h * TH:(h + 1) * TH], start=True, stop=True)
                if kind == "x1tok":
                    pe.wait_ge(x1_ready, h + 1)
                    return turn4(ps, lambda i: x1T[:, h * BH + i * UB:h * BH + (i + 1) * UB, :])
                if kind == "xn2T":
                    wait_taken(pe, ("x1tok", h))
                    return turn4(ps, lambda i: xn_tok[:, h * UH + i, :])
                if kind == "mlp1":
                    j = name[2]
                    wait_taken(pe, ("xn2T", h))
                    return pe.matmul(ps[:, :], w_mlp1_sb[:, j, :], xm2[:, bs, :], start=True, stop=True)
                if kind == "mlp2":
                    for j in range(NJ):
                        wait_taken(pe, ("mlp1", h, j))
                        ins = pe.matmul(ps[:, :], w_mlp2_sb[:, j, :], hidden[:, j, :], start=(j == 0), stop=(j == NJ - 1))
                    return ins
                if kind == "rowsum":
                    pe.wait_ge(consts_ready, 1)
                    pe.wait_ge(x2_ready, h + 1)
                    return pe.matmul(ps[:, :], ones[:, :], x2T[:, bs, :], start=True, stop=True)
                if kind == "self":
                    pe.wait_ge(x2_ready, h + 1)
                    return pe.matmul(ps[:, :], w_cols[:, W_SELF_X, :], x2T[:, bs, :], start=True, stop=True)
                if kind == "q1":
                    wait_taken(pe, ("self", h))
                    return pe.matmul(ps[:, :], w_cols[:, W_Q + name[2], :], selfT[:, bs, :], start=True, stop=True)
                if kind == "k1":
                    return pe.matmul(ps[:, 0:BH * M], w_cols[:, W_K + name[2], :], selfT[:, bs, 0:M], start=True, stop=True)
                if kind == "v1":
                    for u in range(UH):
                        b0 = (h * UH + u) * UB
                        ins = pe.matmul(ps[:, u * P:(u + 1) * P], selfT[:, b0:b0 + UB, :],
                                        w_cols[:, W_OUT + name[2], :], start=True, stop=True)
                    return ins
                if kind == "yfT":
                    g0, g1 = ENDS[h]
                    pe.wait_ge(ysum_ready, h + 1)
                    return turn4(ps, lambda i: y_dir[0][:, g0 + i, :], g1 - g0)
                assert kind == "out"
                g0, g1 = ENDS[h]
                pe.wait_ge(outT_ready, h + 1)
                return turn4(ps, lambda i: outT[:, (g0 + i) * UB:(g0 + i + 1) * UB, :], g1 - g0)

            for stage, i in ORDER:
                if stage == "dense":
                    dense_product(i).then_inc(dense_ready, 1)
                elif stage == "scores":
                    layer, d, g = UNITS[i]
                    h = g // UH
                    for name in ("q", "k") if layer == 0 else ("q1", "k1"):
                        wait_taken(pe, (name, h) + (d,) * layer)
                    if ("q1", h, d) in POOL_Q and layer:
                        pe.wait_ge(q_masked, H4 * POOL_Q.index(("q1", h, d)) + H4)
                    if i >= 2:
                        pe.wait_ge(*((scores_read, i - 1 - N0) if UNITS[i - 2][0] else (shifted, i - 1)))
                    nk = M if layer else S
                    for b in range(UB):
                        ins = pe.matmul(ps_s[i % 2][:, b * P:b * P + HQ * nk], Qm[d][:, g * UB + b, :, :],
                                        Kz[d][:, g * UB + b, :, 0:nk], start=True, stop=True)
                    ins.then_inc(scores_ready, 1)
                elif stage == "turn":
                    layer, d, g = UNITS[i]
                    pe.wait_ge(exp_ready, i + 1)
                    if i >= 1:
                        pe.wait_ge(pt_ready, i)
                    E = E1 if layer else E0
                    for b in range(UB):
                        ins = pe.transpose(ps_t[:, b * P:(b + 1) * P], E[:, i % 3, b * HQ:(b + 1) * HQ, :],
                                           ident[:, :])
                    ins.then_inc(turned, 1)
                elif stage == "values":
                    layer, d, g = UNITS[i]
                    pe.wait_ge(pt_ready, i + 1)
                    wait_taken(pe, (("v1", g // UH, d) if layer else ("v", g // UH)))
                    if i >= 2:
                        pe.wait_ge(y_ready, i - 1)
                    for h4 in range(H4):
                        for b in range(UB):
                            ins = pe.matmul(ps_y[i % 2][QUAD * b:QUAD * b + QUAD, h4 * VW:(h4 + 1) * VW],
                                            PT[:, i % 2, b, h4 * S:(h4 + 1) * S], Vz[d][:, g * UB + b, h4, :],
                                            start=True, stop=True)
                    ins.then_inc(values_ready, 1)

        @block.scalar
        def _(act):
            act.dma_start(x_tok[:, 0:UH, :], x_dram[:, 0:UH, :]).then_inc(ld["x0"], 16)
            act.dma_start(x_tok[:, UH:G, :], x_dram[:, UH:G, :]).then_inc(ld["x1"], 16)
            act.dma_start(xT[:, :, :], xT_dram.rearrange("p (b s) -> p b s", s=S)).then_inc(ld["xT"], 16)
            act.wait_ge(ld["cols"], 16)
            act.activation(silu_t[:, 0, :], cols[:, R_COND:R_COND + B], ACT.Exp, scale=-1.0).then_inc(silu_e, 1)

            def take_part(name, part):
                ps = psum_of(name)
                act.wait_ge(dense_ready, DENSE.index(name) + 1)
                kind, h = (name, 0) if isinstance(name, str) else name[0:2]
                bs = slice(h * BH, (h + 1) * BH)
                if kind == "k":
                    act.wait_ge(kz_ready, h + 1)
                    for hq in (2 * part, 2 * part + 1):
                        q = slice(QUAD * hq, QUAD * hq + QUAD)
                        ins = act.activation(Kz[0][q, bs, hq, :], ps[q, :].rearrange("p (b k) -> p b k", k=S), ACT.Copy)
                    return ins
                if kind == "k1":
                    d = name[2]
                    if d == 1 and h == 0:
                        act.wait_ge(kz1_ready, 1)
                    for hq in (2 * part, 2 * part + 1):
                        q = slice(QUAD * hq, QUAD * hq + QUAD)
                        ins = act.activation(Kz[d][q, bs, hq, 0:M], ps[q, 0:BH * M].rearrange("p (b k) -> p b k", k=M),
                                             ACT.Identity, bias=cols[q, R_K + d:R_K + d + 1])
                    return ins
                if kind in ("v", "v1"):
                    d = name[2] if kind == "v1" else 0
                    nk = M if kind == "v1" else S
                    act.wait_ge(vz_ready[d], HQ * ((h + 1) if kind == "v" else 1 if d else HALVES))
                    for b in (part,):
                        for hq in range(HQ):
                            src = ps[QUAD * b:QUAD * b + nk, :].rearrange("p (u q h c) -> p u q h c", u=UH, q=HQ, h=H4)
                            ins = act.activation(
                                Vz[d][QUAD * hq:QUAD * hq + nk, h * BH + b:(h + 1) * BH:UB, :, hq * C:(hq + 1) * C],
                                src[:, :, hq, :, :], ACT.Copy)
                    return ins
                if kind == "qz":
                    return act.activation(qz[:, :], ps[:, 0:B], ACT.Copy)
                if kind == "yT":
                    return act.activation(yT[:, h * TH:(h + 1) * TH], ps[:, :], ACT.Copy)
                if kind == "mlp1":
                    j = name[2]
                    return act.activation(hidden[:, j, :], ps[:, :], ACT.Gelu_apprx_tanh,
                                          bias=cols[:, R_MLP1 + j:R_MLP1 + j + 1])
                if kind == "q":
                    act.wait_ge(masks_ready, 1)
                    return act.activation(Qm[0][:, bs, part, :], ps[:, :].rearrange("p (b q) -> p b q", q=S), ACT.Copy,
                                          scale=head_mask[:, 0, part:part + 1])
                if name in POOL_Q:
                    n = POOL_Q.index(name)
                    if n >= 2:
                        act.wait_ge(q_masked, H4 * (n - 1))
                    return act.activation(q_flat[:, n % 2, :, :], ps[:, :].rearrange("p (b q) -> p b q", q=S),
                                          ACT.Identity, bias=cols[:, R_Q + name[2]:R_Q + name[2] + 1])
                if kind == "q1":
                    d, h4 = name[2], part
                    act.wait_ge(masks_ready, 2)
                    return act.activation(Qm[d][:, bs, h4, :], ps[:, :].rearrange("p (b q) -> p b q", q=S),
                                          ACT.Identity, scale=head_mask[:, 1, h4:h4 + 1],
                                          bias=bq_masked[:, d, h4:h4 + 1])
                assert kind == "out"
                g0, g1 = ENDS[h]
                return act.activation(out_tok[:, g0:g1, :], ps[:, 0:(g1 - g0) * P].rearrange("p (u f) -> p u f", f=P),
                                      ACT.Copy)

            act.wait_ge(ld["adj"], 16)
            act.activation(adj_f[:, :, :, :].rearrange("p g j l -> p g (j l)"), adj_i[:, :, :], ACT.Copy)\
               .then_inc(adj_ready, 1)
            for stage, i in ORDER:
                if stage == "take" and by_act(*i):
                    ins = take_part(*i)
                    if is_last_part(*i):
                        ins.then_inc(dense_act, 1)
                elif stage == "exp":
                    E, nk = (E1, M) if UNITS[i][0] else (E0, S)
                    act.wait_ge(shifted, i + 1)
                    act.activation(E[:, i % 3, :, 0:nk], E[:, i % 3, :, 0:nk], ACT.Exp).then_inc(exp_ready, 1)
                elif stage == "copy":
                    act.wait_ge(turned, i + 1)
                    if i >= 2:
                        act.wait_ge(values_ready, i - 1)
                    act.activation(PT[:, i % 2, :, :], ps_t[:, :].rearrange("p (b t) -> p b t", t=P), ACT.Copy)\
                       .then_inc(pt_ready, 1)

        @block.vector
        def _(dve):
            count = [0]

            def wait_own(ins):
                count[0] += 1
                ins.then_inc(own, 1)
                dve.wait_ge(own, count[0])

            def norm_stats(layer, h, src):
                gs = slice(h * UH, (h + 1) * UH)
                for i in range(UH):
                    ins = dve.bn_stats(stats[:, h * UH + i, :], src(i))
                wait_own(ins)
                for i in range(UH):
                    ins = dve.bn_aggr(meanvar[:, h * UH + i, :], stats[:, h * UH + i, :])
                wait_own(ins)
                dve.tensor_scalar(var_eps[:, gs], meanvar[:, gs, 1], LN_EPS, None, ALU.add).then_inc(var_ready, 1)

            def norm_apply(layer, h, src):
                dve.wait_ge(rstd_ready, HALVES * layer + h + 1)
                for i in range(UH):
                    g = h * UH + i
                    ins = dve.tensor_scalar(xn_tok[:, g, :], src(i), meanvar[:, g, 0:1], rstd[:, layer, g:g + 1],
                                            ALU.subtract, ALU.mult)
                return ins

            def modulate(dst, ps, shift, scale, bs):
                wait_own(dve.tensor_tensor(dst[:, bs, :], ps[:, :].rearrange("p (b s) -> p b s", s=S),
                                           cmod[:, scale, bs].unsqueeze(2).broadcast_to([P, BH, S]), ALU.mult))
                return dve.tensor_tensor(dst[:, bs, :], dst[:, bs, :],
                                         cmod[:, shift, bs].unsqueeze(2).broadcast_to([P, BH, S]), ALU.add)

            def gated_residual(dst, ps, bias, gate, res, bs):
                ins = dve.scalar_tensor_tensor(out=gated[:, bs, :], in0=ps[:, :].rearrange("p (b s) -> p b s", s=S),
                                               scalar=cols[:, bias:bias + 1],
                                               in1=cmod[:, gate, bs].unsqueeze(2).broadcast_to([P, BH, S]),
                                               op0=ALU.add, op1=ALU.mult)
                ins.then_inc(dense_dve, 1)
                dve.wait_ge(dense_dve, dve_taken[0] + 1)
                return dve.tensor_tensor(dst[:, bs, :], gated[:, bs, :], res[:, bs, :], ALU.add)

            dve_taken = [0]

            def silu():
                dve.wait_ge(silu_e, 1)
                wait_own(dve.tensor_scalar(silu_t[:, 1, :], silu_t[:, 0, :], 1.0, None, ALU.add))
                wait_own(dve.reciprocal(silu_t[:, 0, :], silu_t[:, 1, :]))
                dve.tensor_tensor(silu_c[:, :], silu_t[:, 0, :], cols[:, R_COND:R_COND + B], ALU.mult)\
                   .then_inc(silu_ready, 1)
                for j in (1, 4):
                    ins = dve.tensor_scalar(cols[:, R_ADA + j:R_ADA + j + 1], cols[:, R_ADA + j:R_ADA + j + 1], 1.0,
                                            None, ALU.add)
                wait_own(ins)

            def graph_biases():
                dve.tensor_tensor(bout_sum[:, :], cols[:, R_OUT:R_OUT + 1], cols[:, R_OUT + 1:R_OUT + 2], ALU.add)
                for d in range(DIRS):
                    ins = dve.tensor_scalar(bq_masked[:, d, :], head_mask[:, 1, :], cols[:, R_Q + d:R_Q + d + 1], None,
                                            ALU.mult)
                ins.then_inc(masks_ready, 1)

            def head_masks():
                dve.wait_ge(ident_ready, 1)
                wait_own(dve.tensor_reduce(head_mask[:, 2, :], ident[:, :].rearrange("p (q h c) -> p h q c", q=HQ, h=H4),
                                           AX.XY, ALU.add))
                dve.tensor_scalar(head_mask[:, 1, :], head_mask[:, 2, :], C ** -0.5, None, ALU.mult)
                dve.tensor_scalar(head_mask[:, 0, :], head_mask[:, 2, :], 1.0 / C, None, ALU.mult)\
                   .then_inc(masks_ready, 1)
                dve.wait_ge(masks_ready, 1)

            def edge_bias():
                dve.wait_ge(labels_ready, 1)
                wait_own(dve.tensor_scalar(masked[:, :, :], label_sum[:, :, :], 0.0, NEG, ALU.is_le, ALU.mult))
                dve.scalar_tensor_tensor(out=bias_dir[:, 0, :, :], in0=label_bias[:, :, :], scalar=bb[:, 0:1],
                                         in1=masked[:, :, :], op0=ALU.add, op1=ALU.add).then_inc(bias_ready, 1)
                dve.wait_ge(bias_ready, 1)
                dve.transpose(bias_dir[:, 1, :, :], bias_dir[:, 0, :, :]).then_inc(bias_ready, 1)

            def take_part(name, part):
                ps = psum_of(name)
                dve.wait_ge(dense_ready, DENSE.index(name) + 1)
                kind, h = (name, 0) if isinstance(name, str) else name[0:2]
                bs = slice(h * BH, (h + 1) * BH)
                ps_bs = ps[:, :].rearrange("p (b s) -> p b s", s=S)
                if kind == "cmod":
                    j0, j1 = ADA_CHUNKS[h]
                    dve.tensor_tensor(cmod[:, j0:j1, :], ps[:, j0 * B:j1 * B].rearrange("p (j b) -> p j b", b=B),
                                      cols[:, R_ADA + j0:R_ADA + j1].unsqueeze(2).broadcast_to([P, j1 - j0, B]), ALU.add)\
                       .then_inc(dense_dve, 1)
                    dve.wait_ge(dense_dve, dve_taken[0] + 1)
                elif kind == "xnT":
                    modulate(xm, ps, 0, 1, bs).then_inc(dense_dve, 1)
                elif kind == "q":
                    ins = dve.tensor_scalar(Qm[0][:, bs, part, :], ps_bs, head_mask[:, 0, part:part + 1], None, ALU.mult)
                    if is_last_part(name, part):
                        ins.then_inc(dense_dve, 1)
                elif kind == "proj":
                    if h == 0:
                        dve.wait_ge(ld["xT"], 16)
                    gated_residual(x1T, ps, R_PROJ, 2, xT, bs).then_inc(x1_ready, 1)
                elif kind == "x1tok":
                    if part == 0:
                        norm_stats(1, h, lambda i: ps[:, i * P:(i + 1) * P])
                    else:
                        norm_apply(1, h, lambda i: ps[:, i * P:(i + 1) * P]).then_inc(dense_dve, 1)
                elif kind == "xn2T":
                    modulate(xm2, ps, 3, 4, bs).then_inc(dense_dve, 1)
                elif kind == "mlp2":
                    dve.wait_ge(x1_ready, h + 1)
                    gated_residual(x2T, ps, R_MLP2, 5, x1T, bs).then_inc(x2_ready, 1)
                elif kind == "rowsum":
                    wait_taken(dve, "qz")
                    dve.scalar_tensor_tensor(out=zeroed_q[:, :, :], in0=ps_bs, scalar=0.0,
                                             in1=qz[:, bs].unsqueeze(2).broadcast_to([P, BH, S]),
                                             op0=ALU.not_equal, op1=ALU.mult).then_inc(dense_dve, 1)
                    dve.wait_ge(dense_dve, dve_taken[0] + 1)
                elif kind == "self":
                    dve.scalar_tensor_tensor(out=selfT[:, bs, :], in0=ps_bs, scalar=cols[:, R_SELF:R_SELF + 1],
                                             in1=zeroed_q[:, :, :], op0=ALU.add, op1=ALU.add).then_inc(dense_dve, 1)
                elif kind in ("k", "k1"):
                    d, nk = (0, S) if kind == "k" else (name[2], M)
                    if kind == "k":
                        dve.wait_ge(kz_ready, h + 1)
                    elif d == 1:
                        dve.wait_ge(kz1_ready, 1)
                    for hq in (2 * part, 2 * part + 1):
                        qs = slice(QUAD * hq, QUAD * hq + QUAD)
                        src, dst = ps[qs, 0:BH * nk].rearrange("p (b k) -> p b k", k=nk), Kz[d][qs, bs, hq, 0:nk]
                        if kind == "k":
                            ins = dve.tensor_copy(dst, src)
                        else:
                            ins = dve.tensor_scalar(dst, src, cols[qs, R_K + d:R_K + d + 1], None, ALU.add)
                    if is_last_part(name, part):
                        ins.then_inc(dense_dve, 1)
                elif kind == "q1":
                    d = name[2]
                    ins = dve.tensor_scalar(Qm[d][:, bs, part, :], ps_bs, cols[:, R_Q + d:R_Q + d + 1],
                                            head_mask[:, 1, part:part + 1], ALU.add, ALU.mult)
                    if is_last_part(name, part):
                        ins.then_inc(dense_dve, 1)
                else:
                    assert kind == "yfT"
                    g0, g1 = ENDS[h]
                    bs = slice(g0 * UB, g1 * UB)
                    ps_bs = ps_bs[:, 0:(g1 - g0) * UB, :]
                    dve.scalar_tensor_tensor(out=rT[:, bs, :], in0=ps_bs, scalar=bout_sum[:, 0:1], in1=selfT[:, bs, :],
                                             op0=ALU.add, op1=ALU.add).then_inc(dense_dve, 1)
                    dve.wait_ge(dense_dve, dve_taken[0] + 1)
                    dve.scalar_tensor_tensor(out=outT[:, bs, :], in0=rT[:, bs, :], scalar=0.0, in1=x2T[:, bs, :],
                                             op0=ALU.max, op1=ALU.add).then_inc(outT_ready, 1)
                if is_last_part(name, part):
                    dve_taken[0] += 1

            def softmax_steps(n, m):
                if n is not None:
                    layer, d, g = UNITS[n]
                    nm = neg_max[:, n % 3, :]
                    dve.wait_ge(scores_ready, n + 1)
                    if n >= 3:
                        dve.wait_ge(turned, n - 2)
                    if layer:
                        if n == N0:
                            dve.wait_ge(bias_spread, 16 * H4)
                        e = sc = E1[:, n % 3, :, 0:M]
                        dve.tensor_tensor(e.rearrange("p (b q) k -> p b q k", b=UB),
                                          ps_s[n % 2][:, :].rearrange("p (b r) -> p b r", b=UB)[:, :, 0:HQ * M]
                                          .rearrange("p b (q k) -> p b q k", k=M),
                                          bias_rep[:, d, g * UB:(g + 1) * UB, :].unsqueeze(2)
                                          .broadcast_to([P, UB, HQ, M]), ALU.add).then_inc(scores_read, 1)
                    else:
                        e = E0[:, n % 3, :, :]
                        sc = ps_s[n % 2][:, :].rearrange("p (j k) -> p j k", k=S)
                        dve.tensor_reduce(nm, sc, AX.X, ALU.max, negate=True).then_inc(max_ready, 1)
                if m is not None:
                    dve.wait_ge(values_ready, m + 1)
                    yv = ps_y[m % 2][:, 0:H4 * VW].rearrange("p (h w) -> p h w", w=VW)
                    dve.reciprocal(rden[:, m % 2, :, :], yv[:, :, HQ * C:VW]).then_inc(rden_ready, 1)
                if n is not None and layer:
                    dve.wait_ge(scores_read, n + 1 - N0)
                    dve.tensor_reduce(nm, sc, AX.X, ALU.max, negate=True).then_inc(max_ready, 1)
                if m is not None:
                    m_layer, m_d, m_g = UNITS[m]
                    dst = y_dir[m_d][:, m_g, :] if m_layer else y_tok[:, m_g, :]
                    dve.wait_ge(rden_ready, m + 1)
                    dve.tensor_tensor(dst.rearrange("p (q h c) -> p h q c", q=HQ, h=H4),
                                      yv[:, :, 0:HQ * C].rearrange("p h (q c) -> p h q c", c=C),
                                      rden[:, m % 2, :, :].unsqueeze(3).broadcast_to([P, H4, HQ, C]), ALU.mult)\
                       .then_inc(y_ready, 1)
                if n is not None and not (layer and SUB_POOL):
                    dve.wait_ge(max_ready, n + 1)
                    dve.tensor_tensor(e, sc, nm.unsqueeze(2).broadcast_to([P, UB * HQ, sc.shape[2]]), ALU.add)\
                       .then_inc(shifted, 1)
                if m is not None and m_layer and m_d == 1 and m_g + 1 in [g1 for g0, g1 in ENDS]:
                    gs = slice(*[ends for ends in ENDS if ends[1] == m_g + 1][0])
                    dve.wait_ge(y_ready, m + 1)
                    dve.tensor_tensor(y_dir[0][:, gs, :], y_dir[0][:, gs, :], y_dir[1][:, gs, :], ALU.add)\
                       .then_inc(ysum_ready, 1)

            dve.memset(Kz[0][:, 0:BH, :, :], 0.0).then_inc(kz_ready, 1)
            dve.wait_ge(ld["x0"], 16)
            norm_stats(0, 0, lambda i: x_tok[:, i, :])
            silu()
            norm_apply(0, 0, lambda i: x_tok[:, i, :]).then_inc(xn_ready, 1)
            head_masks()
            for stage, i in ORDER:
                if stage == "take" and not by_act(*i):
                    take_part(*i)
                elif stage == "norm1":
                    if i == 0:
                        dve.wait_ge(ld["x1"], 16)
                        norm_stats(0, 1, lambda i: x_tok[:, UH + i, :])
                        graph_biases()
                    else:
                        norm_apply(0, 1, lambda i: x_tok[:, UH + i, :]).then_inc(xn_ready, 1)
                elif stage == "edges":
                    edge_bias()
                elif stage == "soft":
                    softmax_steps(*i)


def kernel(**inputs):
    import numpy as np
    import concourse.bacc as bacc
    from concourse.bass_utils import run_bass_kernel_spmd

    a = {name: np.asarray(value) for name, value in inputs.items()}
    vectors = [a["cond_1024"]] + [a[n].reshape(-1, P) for n in (
        "L0_cond_b_ada", "L0_cond_b_proj", "L0_cond_b_mlp1", "L0_cond_b_mlp2", "L1_cond_b_self", "L1_cond_bq",
        "L1_cond_bk", "L1_cond_bout")]
    cols = np.concatenate([np.concatenate(vectors).T, np.broadcast_to(a["L1_cond_w_bias"], (P, L)),
                           np.broadcast_to(a["L1_cond_b_bias"], (P, 1))], axis=1)
    x = a["x"]
    w_graph = [a["L1_cond_W_self"].T.reshape(2, P, P)] + [
        a[n].reshape(DIRS, P, P).transpose(0, 2, 1) for n in ("L1_cond_Wq", "L1_cond_Wk", "L1_cond_Wout")]
    arrays = {
        "cols": cols,
        "x_tok": x.reshape(G, UB * S, P).transpose(1, 0, 2),
        "xT": x.reshape(B * S, P).T,
        "adj": a["mask_BxSxSx11_ik0"].reshape(G, UB * S, S * L).transpose(1, 0, 2),
        "w_ada": a["L0_cond_w_ada"],
        "w_qkv": a["L0_cond_w_qkv"],
        "w_rest": np.concatenate([a["L0_cond_w_proj"], a["L0_cond_w_mlp1"],
                                  a["L0_cond_w_mlp2"].reshape(NJ, P, P).transpose(1, 0, 2).reshape(P, NJ * P)]
                                 + [w for ws in w_graph for w in ws], axis=1),
    }
    arrays = {name: np.ascontiguousarray(value) for name, value in arrays.items()}
    nc = bacc.Bacc("TRN2", target_bir_lowering=False, num_devices=1)
    ins = {name: nc.dram_tensor("in_" + name, value.shape, mybir.dt.from_np(value.dtype), kind="ExternalInput").ap()
           for name, value in arrays.items()}
    out = nc.dram_tensor("out_0", (B, S, P), F32, kind="ExternalOutput").ap()
    program(nc, out=out, **ins)
    r = run_bass_kernel_spmd(nc, [{"in_" + name: value for name, value in arrays.items()}], core_ids=[0])
    return r.results[0]["out_0"]
```

```python
from contextlib import ExitStack

import concourse.bass as bass
from concourse import mybir

ALU = mybir.AluOpType
ACT = mybir.ActivationFunctionType
F32 = mybir.dt.float32
I32 = mybir.dt.int32
AX = mybir.AxisListType

P = 128
B = 32
S = 32
QUAD = 32
HQ = 4
H4 = 4
C = 8
G = 8
UB = 4
HALVES = 2
BH = B // HALVES
UH = G // HALVES
TH = BH * S
M = 20
L = 11
NJ = 4
VW = HQ * C + HQ
LN_EPS = 1e-6
NEG = -9000000000000000.0
DIRS = 2

R_COND = 0
R_ADA = B
R_PROJ = R_ADA + 6
R_MLP1 = R_PROJ + 1
R_MLP2 = R_MLP1 + NJ
R_SELF = R_MLP2 + 1
R_Q = R_SELF + 1
R_K = R_Q + DIRS
R_OUT = R_K + DIRS
R_LABEL = R_OUT + DIRS
COLS = R_LABEL + L + 1

UNITS = [(0, 0, g) for g in range(G)]
for _h in range(HALVES):
    for _d in range(DIRS):
        UNITS += [(1, _d, _h * UH + _u) for _u in range(UH)]
N0 = G
POOL_SUBS = range(N0, N0 + 15)
LABEL_STEPS = 4
STARTS = [(0, 2), (2, 4), (4, 8)]
ENDS = [(0, 4), (4, 7), (7, 8)]

PARTS = {"q": 4, "q1": 4, "k": 2, "k1": 2, "v": 4, "v1": 4, "x1tok": 2}


def kind_of(name):
    return name if isinstance(name, str) else name[0]


def parts_of(name):
    return PARTS.get(kind_of(name), 1)


ORDER = [
    ("dense", ("cmod", 0)), ("dense", ("xnT", 0)), ("norm1", (1, 0)), ("take", (("cmod", 0), 0)),
    ("take", (("xnT", 0), 0)), ("norm1", (1, 1)), ("norm1", (2, 0)), ("dense", ("cmod", 1)), ("dense", ("q", 0)),
    ("dense", ("k", 0)), ("take", (("k", 0), 0)), ("take", (("cmod", 1), 0)), ("take", (("q", 0), 3)),
    ("take", (("q", 0), 0)), ("take", (("q", 0), 2)), ("take", (("q", 0), 1)), ("take", (("k", 0), 1)),
    ("dense", ("xnT", 1)), ("labels", 0),
    ("scores", 0), ("take", (("xnT", 1), 0)), ("norm1", (2, 1)), ("labels", 1), ("dense", ("xnT", 2)),
    ("labels", 2), ("soft", (0, None)), ("labels", 3), ("take", (("xnT", 2), 0)), ("exp", 0),
    ("scores", 1), ("dense", ("q", 1)), ("dense", ("k", 1)), ("turn", 0), ("take", (("q", 1), 2)),
    ("take", (("q", 1), 3)), ("take", (("q", 1), 0)), ("take", (("q", 1), 1)), ("soft", (1, None)),
    ("take", (("k", 1), 1)), ("dense", ("k", 2)), ("dense", ("v", 0)), ("take", (("k", 2), 0)), ("exp", 1),
    ("take", (("k", 1), 0)),
    ("scores", 2), ("copy", 0), ("take", (("v", 0), 3)), ("take", (("v", 0), 2)), ("take", (("v", 0), 1)),
    ("take", (("v", 0), 0)), ("take", (("k", 2), 1)), ("dense", ("q", 2)),
    ("scores", 3), ("turn", 1), ("values", 0), ("take", (("q", 2), 0)), ("soft", (2, None)), ("soft", (3, None)),
    ("exp", 2), ("copy", 1), ("take", (("q", 2), 2)), ("soft", (None, 0)), ("take", (("q", 2), 3)),
    ("take", (("q", 2), 1)), ("turn", 2), ("exp", 3), ("copy", 2), ("dense", ("v", 1)), ("values", 1),
    ("soft", (None, 1)), ("take", (("v", 1), 0)), ("values", 2),
    ("scores", 4), ("dense", "qz"), ("turn", 3), ("take", (("v", 1), 1)), ("copy", 3), ("soft", (4, 2)),
    ("scores", 5), ("values", 3), ("soft", (5, 3)),
    ("scores", 6), ("soft", (6, None)), ("exp", 4), ("take", (("v", 1), 3)), ("take", (("v", 1), 2)), ("turn", 4),
    ("dense", ("yT", 0)),
    ("scores", 7), ("exp", 5), ("take", (("yT", 0), 0)), ("take", ("qz", 0)), ("dense", ("proj", 0)),
    ("soft", (7, None)), ("exp", 6), ("copy", 4), ("turn", 5), ("values", 4), ("take", (("proj", 0), 0)),
    ("soft", (None, 4)), ("exp", 7), ("copy", 5), ("turn", 6), ("dense", ("x1tok", 0)), ("copy", 6), ("values", 5),
    ("turn", 7), ("values", 6), ("copy", 7), ("take", (("x1tok", 0), 0)), ("soft", (None, 5)), ("soft", (None, 6)),
    ("values", 7), ("soft", (None, 7)), ("dense", ("yT", 1)), ("take", (("yT", 1), 0)), ("take", (("x1tok", 0), 1)),
    ("dense", ("xn2T", 0)), ("dense", ("proj", 1)), ("edges", 0), ("take", (("xn2T", 0), 0)),
    ("take", (("proj", 1), 0)), ("dense", ("mlp1", 0, 1)), ("dense", ("mlp1", 0, 0)), ("dense", ("x1tok", 1)),
    ("take", (("mlp1", 0, 0), 0)), ("take", (("mlp1", 0, 1), 0)), ("dense", ("mlp1", 0, 3)),
    ("dense", ("mlp1", 0, 2)), ("take", (("mlp1", 0, 3), 0)), ("take", (("mlp1", 0, 2), 0)),
    ("take", (("x1tok", 1), 0)), ("take", (("x1tok", 1), 1)), ("dense", ("xn2T", 1)), ("dense", ("mlp2", 0)),
    ("take", (("xn2T", 1), 0)), ("dense", ("mlp1", 1, 2)), ("take", (("mlp2", 0), 0)), ("dense", ("mlp1", 1, 0)),
    ("take", (("mlp1", 1, 2), 0)), ("dense", ("rowsum", 0)), ("take", (("mlp1", 1, 0), 0)), ("dense", ("self", 0)),
    ("take", (("rowsum", 0), 0)), ("dense", ("mlp1", 1, 1)), ("take", (("self", 0), 0)), ("dense", ("mlp1", 1, 3)),
    ("take", (("mlp1", 1, 1), 0)), ("dense", ("q1", 0, 0)), ("take", (("q1", 0, 0), 0)),
    ("take", (("q1", 0, 0), 3)), ("take", (("mlp1", 1, 3), 0)), ("dense", ("mlp2", 1)), ("dense", ("k1", 0, 0)),
    ("take", (("mlp2", 1), 0)), ("take", (("q1", 0, 0), 1)), ("take", (("q1", 0, 0), 2)), ("dense", ("q1", 0, 1)),
    ("take", (("k1", 0, 0), 0)), ("take", (("k1", 0, 0), 1)), ("dense", ("v1", 0, 0)), ("take", (("q1", 0, 1), 2)),
    ("take", (("q1", 0, 1), 1)), ("take", (("q1", 0, 1), 0)), ("take", (("q1", 0, 1), 3)),
    ("take", (("v1", 0, 0), 3)), ("take", (("v1", 0, 0), 1)), ("take", (("v1", 0, 0), 2)),
    ("take", (("v1", 0, 0), 0)), ("dense", ("rowsum", 1)),
    ("scores", 8), ("soft", (8, None)), ("sub", 8),
    ("scores", 9), ("dense", ("self", 1)), ("soft", (9, None)), ("take", (("rowsum", 1), 0)), ("sub", 9),
    ("exp", 8), ("take", (("self", 1), 0)), ("dense", ("k1", 0, 1)),
    ("scores", 10), ("turn", 8),
    ("scores", 11), ("dense", ("q1", 1, 0)), ("take", (("k1", 0, 1), 1)), ("copy", 8), ("exp", 9), ("values", 8),
    ("turn", 9), ("copy", 9), ("dense", ("v1", 0, 1)), ("soft", (10, None)), ("take", (("k1", 0, 1), 0)),
    ("sub", 10), ("exp", 10),
    ("scores", 12), ("take", (("q1", 1, 0), 1)), ("take", (("q1", 1, 0), 2)), ("take", (("q1", 1, 0), 3)),
    ("soft", (11, None)), ("sub", 11), ("soft", (None, 8)), ("take", (("q1", 1, 0), 0)), ("turn", 10),
    ("scores", 13), ("values", 9), ("dense", ("k1", 1, 0)), ("soft", (12, None)), ("soft", (None, 9)), ("sub", 12),
    ("take", (("v1", 0, 1), 0)), ("dense", ("q1", 1, 1)), ("take", (("v1", 0, 1), 3)), ("copy", 10),
    ("take", (("v1", 0, 1), 1)), ("take", (("v1", 0, 1), 2)), ("take", (("k1", 1, 0), 0)), ("exp", 11),
    ("scores", 14), ("values", 10), ("turn", 11), ("exp", 12), ("copy", 11), ("take", (("q1", 1, 1), 0)),
    ("soft", (13, 10)), ("sub", 13),
    ("scores", 15), ("values", 11), ("turn", 12), ("copy", 12), ("exp", 13), ("take", (("k1", 1, 0), 1)),
    ("dense", ("v1", 1, 0)), ("values", 12), ("turn", 13), ("take", (("v1", 1, 0), 2)), ("take", (("v1", 1, 0), 1)),
    ("soft", (14, 11)), ("sub", 14), ("dense", ("k1", 1, 1)),
    ("scores", 16), ("copy", 13), ("exp", 14), ("take", (("k1", 1, 1), 1)), ("soft", (15, None)), ("sub", 15),
    ("scores", 17), ("turn", 14), ("take", (("q1", 1, 1), 2)), ("soft", (16, 12)), ("take", (("q1", 1, 1), 3)),
    ("take", (("q1", 1, 1), 1)), ("sub", 16),
    ("scores", 18), ("values", 13), ("soft", (17, 13)), ("sub", 17), ("take", (("k1", 1, 1), 0)), ("exp", 15),
    ("copy", 14), ("values", 14), ("turn", 15), ("dense", ("v1", 1, 1)),
    ("scores", 19), ("soft", (18, 14)), ("sub", 18), ("take", (("v1", 1, 0), 0)), ("exp", 16), ("copy", 15),
    ("turn", 16),
    ("scores", 20), ("values", 15), ("soft", (19, 15)), ("sub", 19), ("exp", 17), ("copy", 16),
    ("take", (("v1", 1, 1), 0)), ("turn", 17),
    ("scores", 21), ("take", (("v1", 1, 0), 3)), ("values", 16), ("soft", (20, 16)), ("sub", 20), ("exp", 18),
    ("copy", 17), ("turn", 18), ("take", (("v1", 1, 1), 1)), ("exp", 19), ("take", (("v1", 1, 1), 2)), ("copy", 18),
    ("values", 17),
    ("scores", 22), ("soft", (21, 17)), ("turn", 19), ("sub", 21), ("copy", 19), ("exp", 20),
    ("scores", 23), ("values", 18), ("soft", (22, 18)), ("exp", 21), ("turn", 20), ("sub", 22), ("copy", 20),
    ("take", (("v1", 1, 1), 3)), ("exp", 22), ("dense", ("yfT", 0)), ("values", 19), ("soft", (23, 19)),
    ("turn", 21), ("values", 20), ("copy", 21), ("exp", 23), ("turn", 22), ("values", 21), ("soft", (None, 20)),
    ("take", (("yfT", 0), 0)), ("copy", 22), ("turn", 23), ("values", 22), ("soft", (None, 21)), ("copy", 23),
    ("soft", (None, 22)), ("values", 23), ("dense", ("yfT", 1)), ("dense", ("out", 0)), ("take", (("out", 0), 0)),
    ("soft", (None, 23)), ("take", (("yfT", 1), 0)), ("dense", ("yfT", 2)), ("take", (("yfT", 2), 0)),
    ("dense", ("out", 1)), ("dense", ("out", 2)), ("take", (("out", 1), 0)), ("take", (("out", 2), 0)),
]
DENSE = [i for stage, i in ORDER if stage == "dense"]
TAKES = [i for stage, i in ORDER if stage == "take"]

ACT_PARTS = {"k": (0, 1), "v": (0, 1, 2, 3), "k1": (0, 1), "v1": (0, 1, 2, 3), "qz": (0,), "yT": (0,), "mlp1": (0,),
             "out": (0,), ("q", 0): (0, 1, 2, 3), ("q", 1): (0, 1, 2, 3), ("k1", 0, 0): (0, 1),
             ("q1", 0, 0): (0, 1, 2, 3), ("k", 1): (0,), ("k", 2): (1,), ("k1", 0, 1): (1,), ("k1", 1, 1): (0, 1),
             ("k1", 1, 0): (0,), ("k", 0): (1,)}
ADA_CHUNKS = [(0, 2), (2, 6)]


def by_act(name, part):
    return part in ACT_PARTS.get(name, ACT_PARTS.get(kind_of(name), ()))


def last_takes(act):
    names = [name for name, part in TAKES if by_act(name, part) == act]
    return [n for i, n in enumerate(names) if n not in names[i + 1:]]


def is_last_part(name, part):
    parts = [p for n, p in TAKES if n == name and by_act(n, p) == by_act(name, part)]
    return parts[-1] == part


def program(nc, cols, x_tok, xT, adj, w_ada, w_qkv, w_rest, out):
    x_dram, xT_dram, cols_dram, adj_dram = x_tok, xT, cols, adj
    with ExitStack() as ctx:
        def sb(name, shape, dt=F32):
            return ctx.enter_context(nc.sbuf_tensor(name, shape, dt))

        def sem(name):
            return ctx.enter_context(nc.semaphore(name))

        ident = sb("ident", [P, P])
        ones = sb("ones", [P, P])
        head_mask = sb("head_mask", [P, 3, H4])
        minus_half = sb("minus_half", [P, UH])
        cols = sb("cols", [P, COLS])
        wb = cols[:, R_LABEL:R_LABEL + L]
        bb = cols[:, R_LABEL + L:COLS]
        silu_t = sb("silu_t", [P, 2, B])
        silu_c = sb("silu_c", [P, B])
        cmod = sb("cmod", [P, 6, B])
        bout_sum = sb("bout_sum", [P, 1])
        bq_masked = sb("bq_masked", [P, DIRS, H4])
        qz = sb("qz", [P, B])
        x_tok = sb("x_tok", [P, G, P])
        xn_tok = sb("xn_tok", [P, G, P])
        stats = sb("stats", [P, G, 6])
        meanvar = sb("meanvar", [P, G, 2])
        var_eps = sb("var_eps", [P, G])
        rstd = sb("rstd", [P, 2, G])
        xT = sb("xT", [P, B, S])
        xm = sb("xm", [P, B, S])
        xm2 = xm
        gated = sb("gated", [P, B, S])
        x1T = sb("x1T", [P, B, S])
        x2T = sb("x2T", [P, B, S])
        zeroed_q = sb("zeroed_q", [P, BH, S])
        selfT = sb("selfT", [P, B, S])
        hidden = sb("hidden", [P, NJ, TH])
        y_tok = sb("y_tok", [P, G, P])
        yT = sb("yT", [P, B * S])
        y_dir = [yT[:, :].rearrange("p (g f) -> p g f", f=P), y_tok[:, :, :]]
        Qm = [sb(f"Qm{d}", [P, B, H4, S]) for d in range(DIRS)]
        Kz = [sb(f"Kz{d}", [P, B, HQ, S]) for d in range(DIRS)]
        Vz = [sb(f"Vz{d}", [P, B, H4, VW]) for d in range(DIRS)]
        E0 = sb("E0", [P, 3, UB * HQ, S])
        E1 = sb("E1", [P, 3, UB * HQ, S])
        PT = sb("PT", [P, 2, UB, P])
        neg_max = sb("neg_max", [P, 3, UB * HQ])
        rden = sb("rden", [P, 2, H4, HQ])
        w_ada_sb = sb("w_ada_sb", [P, 6 * P])
        w_qkv_sb = sb("w_qkv_sb", [P, 3 * P])
        w_rest_sb = sb("w_rest_sb", [P, 17, P])
        w_proj_sb = w_rest_sb[:, 0, :]
        w_mlp1_sb = w_rest_sb[:, 1:1 + NJ, :]
        w_mlp2_sb = w_rest_sb[:, 5:5 + NJ, :]
        w_cols = w_rest_sb[:, 9:17, :]
        adj_i = Qm[1][:, :, :, :].rearrange("p b h s -> p (b h s)")[:, 0:G * S * L].bitcast(I32)\
            .rearrange("p (g r) -> p g r", g=G)
        adj_f = sb("adj_f", [P, G, S, L])
        label_sum = sb("label_sum", [P, G, S])
        label_bias = sb("label_bias", [P, G, S])
        masked = sb("masked", [P, G, S])
        bias_dir = sb("bias_dir", [P, DIRS, G, S])
        bias_rep = sb("bias_rep", [P, DIRS, B, M])
        bias_dram = nc.dram_tensor("bias_dram", (S, DIRS, B, M), F32, kind="Internal").ap()
        out_tok = x_tok
        outT = x1T
        rT = gated
        W_SELF_X, W_SELF_Q, W_Q, W_K, W_OUT = 0, 1, 2, 4, 6

        def bank(name):
            return ctx.enter_context(nc.psum_tensor(name, [P, 512], F32))
        ps_s = [bank(f"ps_s{i}") for i in range(2)]
        ps_t = bank("ps_t")
        ps_y = [bank(f"ps_y{i}") for i in range(2)]
        ps_d = [bank(f"ps_d{i}") for i in range(3)]

        ld = {n: sem("ld_" + n) for n in ("cols", "x0", "x1", "ada", "qkv", "xT", "adj", "rest")}
        stored = sem("stored")
        ident_ready = sem("ident_ready")
        consts_ready = sem("consts_ready")
        kz_ready = sem("kz_ready")
        kz1_ready = sem("kz1_ready")
        vz_ready = [sem(f"vz_ready{d}") for d in range(DIRS)]
        dense_ready = sem("dense_ready")
        dense_act = sem("dense_act")
        dense_dve = sem("dense_dve")
        scores_ready = sem("scores_ready")
        scores_read = sem("scores_read")
        shifted = sem("shifted")
        shifted_pool = sem("shifted_pool")
        exp_ready = sem("exp_ready")
        max_ready = sem("max_ready")
        rden_ready = sem("rden_ready")
        masks_ready = sem("masks_ready")
        turned = sem("turned")
        pt_ready = sem("pt_ready")
        values_ready = sem("values_ready")
        y_ready = sem("y_ready")
        own = sem("own")
        var_ready = sem("var_ready")
        rstd_ready = sem("rstd_ready")
        xn_ready = sem("xn_ready")
        x1_ready = sem("x1_ready")
        x2_ready = sem("x2_ready")
        silu_e = sem("silu_e")
        silu_ready = sem("silu_ready")
        ysum_ready = sem("ysum_ready")
        outT_ready = sem("outT_ready")
        adj_ready = sem("adj_ready")
        labels_ready = sem("labels_ready")
        pool_own = sem("pool_own")
        bias_ready = sem("bias_ready")
        bias_out = sem("bias_out")
        bias_spread = sem("bias_spread")

        def wait_taken(engine, name):
            for sem_taken, act in ((dense_act, True), (dense_dve, False)):
                names = last_takes(act)
                if name in names:
                    engine.wait_ge(sem_taken, names.index(name) + 1)

        def rstd_count(layer, g0):
            return len(STARTS) + g0 // UH + 1 if layer else [first for first, _ in STARTS].index(g0) + 1

        def shift_of(n):
            mine = n in POOL_SUBS
            return (shifted_pool if mine else shifted), sum((m in POOL_SUBS) == mine for m in range(n + 1))

        def psum_of(name):
            return ps_d[DENSE.index(name) % len(ps_d)]

        block = ctx.enter_context(nc.Block())

        @block.sync
        def _(sp):
            sp.dma_start(cols[:, :], cols_dram).then_inc(ld["cols"], 16)
            sp.dma_start(w_ada_sb[:, :], w_ada).then_inc(ld["ada"], 16)
            sp.dma_start(w_qkv_sb[:, :], w_qkv).then_inc(ld["qkv"], 16)
            sp.dma_start(adj_i[:, :, :], adj_dram).then_inc(ld["adj"], 16)
            sp.dma_start(w_rest_sb[:, :, :], w_rest.rearrange("p (j o) -> p j o", o=P)).then_inc(ld["rest"], 16)
            sp.wait_ge(bias_ready, 2)
            for b in range(UB):
                sp.dma_start(bias_dram[:, :, b:B:UB, :], bias_dir[QUAD * b:QUAD * b + QUAD, :, :, 0:M])\
                  .then_inc(bias_out, 16)
            sp.wait_ge(bias_out, 16 * UB)
            for h4 in range(H4):
                sp.dma_start(bias_rep[QUAD * h4:QUAD * h4 + QUAD, :, :, :], bias_dram).then_inc(bias_spread, 16)
            o_v = out.rearrange("(g b) s f -> (b s) g f", b=UB)
            for e, (g0, g1) in enumerate(ENDS):
                wait_taken(sp, ("out", e))
                sp.dma_start(o_v[:, g0:g1, :], out_tok[:, g0:g1, :]).then_inc(stored, 16)
            sp.wait_ge(stored, 16 * len(ENDS))

        @block.gpsimd
        def _(pool):
            pool.memset(ident[:, :], 0.0).then_inc(pool_own, 1)
            pool.wait_ge(pool_own, 1)
            pool.affine_select(out=ident[:, :], in_=ident[:, :], compare_op=ALU.not_equal, fill=1.0, base=0,
                               pattern=[[-1, P]], channel_multiplier=1).then_inc(ident_ready, 1)
            pool.memset(minus_half[:, :], -0.5).then_inc(pool_own, 1)

            def ones_block(d, bs):
                for hq in range(HQ):
                    pool.memset(Vz[d][QUAD * hq:QUAD * hq + QUAD, bs, :, HQ * C + hq], 1.0).then_inc(vz_ready[d], 1)

            def rstd_of(layer, g0, g1):
                pool.wait_ge(var_ready, rstd_count(layer, g0))
                pool.tensor_tensor(rstd[:, layer, g0:g1], var_eps[:, g0:g1], minus_half[:, 0:g1 - g0], ALU.pow)\
                    .then_inc(rstd_ready, 1)

            pool.memset(Vz[0][:, 0:BH, :, :], 0.0).then_inc(pool_own, 1)
            pool.wait_ge(pool_own, 3)
            rstd_of(0, *STARTS[0])
            rstd_of(0, *STARTS[1])
            pool.wait_ge(rstd_ready, 2)
            ones_block(0, slice(0, BH))
            pool.wait_ge(vz_ready[0], HQ)
            pool.memset(Kz[0][:, BH:B, :, :], 0.0).then_inc(kz_ready, 1)
            rstd_of(0, *STARTS[2])
            pool.memset(Vz[0][:, BH:B, :, :], 0.0).then_inc(pool_own, 1)
            pool.wait_ge(pool_own, 4)
            pool.wait_ge(rstd_ready, 3)
            ones_block(0, slice(BH, B))
            pool.wait_ge(vz_ready[0], HALVES * HQ)
            pool.memset(E1[:, :, :, M:S], 0.0)
            pool.memset(ones[:, :], 1.0).then_inc(consts_ready, 1)
            own_n = 4
            pool.wait_ge(adj_ready, LABEL_STEPS)
            for l in range(1, L):
                a = adj_f[:, :, :, 0] if l == 1 else label_sum[:, :, :]
                if l > 1:
                    pool.wait_ge(pool_own, own_n)
                pool.tensor_tensor(label_sum[:, :, :], a, adj_f[:, :, :, l], ALU.add).then_inc(pool_own, 1)
                own_n += 1
            pool.wait_ge(ld["cols"], 16)
            pool.wait_ge(pool_own, own_n)
            for g in range(0, G, 2):
                flat = adj_f[:, g:g + 2, :, :].rearrange("p g j l -> p (g j) l")
                pool.tensor_tensor(flat, flat, wb.unsqueeze(1).broadcast_to([P, 2 * S, L]), ALU.mult)\
                    .then_inc(pool_own, 1)
                own_n += 1
            for l in range(1, L):
                a = adj_f[:, :, :, 0] if l == 1 else label_bias[:, :, :]
                pool.wait_ge(pool_own, own_n)
                ins = pool.tensor_tensor(label_bias[:, :, :], a, adj_f[:, :, :, l], ALU.add)
                if l == L - 1:
                    ins.then_inc(labels_ready, 1)
                else:
                    ins.then_inc(pool_own, 1)
                own_n += l < L - 1
            rstd_of(1, 0, UH)
            pool.memset(Kz[1][:, :, :, :], 0.0).then_inc(kz1_ready, 1)
            pool.memset(Vz[1][:, :, :, :], 0.0).then_inc(pool_own, 1)
            own_n += 1
            pool.wait_ge(pool_own, own_n)
            ones_block(1, slice(0, B))
            pool.wait_ge(vz_ready[1], HQ)

            rstd_of(1, UH, G)
            for stage, i in ORDER:
                if stage == "sub":
                    pool.wait_ge(max_ready, i + 1)
                    e, nm = E1[:, i % 3, :, 0:M], neg_max[:, i % 3, :]
                    pool.tensor_tensor(e, e, nm.unsqueeze(2).broadcast_to([P, UB * HQ, M]), ALU.add)\
                        .then_inc(shifted_pool, 1)

        @block.tensor
        def _(pe):
            def turn4(ps, src, count=4):
                for i in range(count):
                    ins = pe.transpose(ps[:, i * P:(i + 1) * P], src(i), ident[:, :])
                return ins

            def dense_product(name):
                ps = psum_of(name)
                k = DENSE.index(name)
                if k >= len(ps_d):
                    wait_taken(pe, DENSE[k - len(ps_d)])
                kind, h = (name, 0) if isinstance(name, str) else name[0:2]
                if kind in ("xnT", "q", "k"):
                    g0, g1 = STARTS[h]
                    bs = slice(g0 * UB, g1 * UB)
                else:
                    bs = slice(h * BH, (h + 1) * BH)
                if kind == "cmod":
                    pe.wait_ge(ld["ada"], 16)
                    pe.wait_ge(silu_ready, 1)
                    for j in range(*ADA_CHUNKS[h]):
                        ins = pe.matmul(ps[:, j * B:(j + 1) * B], w_ada_sb[:, j * P:(j + 1) * P], silu_c[:, :],
                                        start=True, stop=True)
                    return ins
                if kind == "xnT":
                    if h == 0:
                        pe.wait_ge(ident_ready, 1)
                    pe.wait_ge(xn_ready, h + 1)
                    return turn4(ps, lambda i: xn_tok[:, g0 + i, :], g1 - g0)
                if kind in ("q", "k"):
                    pe.wait_ge(ld["qkv"], 16)
                    wait_taken(pe, ("xnT", h))
                    w = w_qkv_sb[:, P:2 * P] if kind == "q" else w_qkv_sb[:, 0:P]
                    return pe.matmul(ps[:, 0:(g1 - g0) * P], w, xm[:, bs, :], start=True, stop=True)
                if kind == "v":
                    pe.wait_ge(ld["qkv"], 16)
                    for c, (g0, g1) in enumerate(STARTS):
                        if g0 // UH == h:
                            wait_taken(pe, ("xnT", c))
                    for u in range(UH):
                        b0 = (h * UH + u) * UB
                        ins = pe.matmul(ps[:, u * P:(u + 1) * P], xm[:, b0:b0 + UB, :], w_qkv_sb[:, 2 * P:3 * P],
                                        start=True, stop=True)
                    return ins
                if kind == "qz":
                    pe.wait_ge(ld["rest"], 16)
                    return pe.matmul(ps[:, 0:B], w_cols[:, W_SELF_Q, :], cols[:, R_COND:R_COND + B], start=True,
                                     stop=True)
                if kind == "yT":
                    pe.wait_ge(y_ready, (h + 1) * UH)
                    return turn4(ps, lambda i: y_tok[:, h * UH + i, :])
                if kind == "proj":
                    pe.wait_ge(ld["rest"], 16)
                    wait_taken(pe, ("yT", h))
                    return pe.matmul(ps[:, :], w_proj_sb, yT[:, h * TH:(h + 1) * TH], start=True, stop=True)
                if kind == "x1tok":
                    pe.wait_ge(x1_ready, h + 1)
                    return turn4(ps, lambda i: x1T[:, h * BH + i * UB:h * BH + (i + 1) * UB, :])
                if kind == "xn2T":
                    wait_taken(pe, ("x1tok", h))
                    return turn4(ps, lambda i: xn_tok[:, h * UH + i, :])
                if kind == "mlp1":
                    j = name[2]
                    wait_taken(pe, ("xn2T", h))
                    return pe.matmul(ps[:, :], w_mlp1_sb[:, j, :], xm2[:, bs, :], start=True, stop=True)
                if kind == "mlp2":
                    for j in range(NJ):
                        wait_taken(pe, ("mlp1", h, j))
                        ins = pe.matmul(ps[:, :], w_mlp2_sb[:, j, :], hidden[:, j, :], start=(j == 0),
                                        stop=(j == NJ - 1))
                    return ins
                if kind == "rowsum":
                    pe.wait_ge(consts_ready, 1)
                    pe.wait_ge(x2_ready, h + 1)
                    return pe.matmul(ps[:, :], ones[:, :], x2T[:, bs, :], start=True, stop=True)
                if kind == "self":
                    pe.wait_ge(x2_ready, h + 1)
                    return pe.matmul(ps[:, :], w_cols[:, W_SELF_X, :], x2T[:, bs, :], start=True, stop=True)
                if kind == "q1":
                    wait_taken(pe, ("self", h))
                    return pe.matmul(ps[:, :], w_cols[:, W_Q + name[2], :], selfT[:, bs, :], start=True, stop=True)
                if kind == "k1":
                    return pe.matmul(ps[:, 0:BH * M], w_cols[:, W_K + name[2], :], selfT[:, bs, 0:M], start=True,
                                     stop=True)
                if kind == "v1":
                    for u in range(UH):
                        b0 = (h * UH + u) * UB
                        ins = pe.matmul(ps[:, u * P:(u + 1) * P], selfT[:, b0:b0 + UB, :],
                                        w_cols[:, W_OUT + name[2], :], start=True, stop=True)
                    return ins
                if kind == "yfT":
                    g0, g1 = ENDS[h]
                    pe.wait_ge(ysum_ready, h + 1)
                    return turn4(ps, lambda i: y_dir[0][:, g0 + i, :], g1 - g0)
                assert kind == "out"
                g0, g1 = ENDS[h]
                pe.wait_ge(outT_ready, h + 1)
                return turn4(ps, lambda i: outT[:, (g0 + i) * UB:(g0 + i + 1) * UB, :], g1 - g0)

            for stage, i in ORDER:
                if stage == "dense":
                    dense_product(i).then_inc(dense_ready, 1)
                elif stage == "scores":
                    layer, d, g = UNITS[i]
                    h = g // UH
                    c = [g0 <= g < g1 for g0, g1 in STARTS].index(True)
                    for name in (("q1", h, d), ("k1", h, d)) if layer else (("q", c), ("k", c)):
                        wait_taken(pe, name)
                    if i >= 2:
                        pe.wait_ge(*((scores_read, i - 1 - N0) if UNITS[i - 2][0] else shift_of(i - 2)))
                    nk = M if layer else S
                    for b in range(UB):
                        ins = pe.matmul(ps_s[i % 2][:, b * P:b * P + HQ * nk], Qm[d][:, g * UB + b, :, :],
                                        Kz[d][:, g * UB + b, :, 0:nk], start=True, stop=True)
                    ins.then_inc(scores_ready, 1)
                elif stage == "turn":
                    layer, d, g = UNITS[i]
                    pe.wait_ge(exp_ready, i + 1)
                    if i >= 1:
                        pe.wait_ge(pt_ready, i)
                    E = E1 if layer else E0
                    for b in range(UB):
                        ins = pe.transpose(ps_t[:, b * P:(b + 1) * P], E[:, i % 3, b * HQ:(b + 1) * HQ, :],
                                           ident[:, :])
                    ins.then_inc(turned, 1)
                elif stage == "values":
                    layer, d, g = UNITS[i]
                    pe.wait_ge(pt_ready, i + 1)
                    wait_taken(pe, (("v1", g // UH, d) if layer else ("v", g // UH)))
                    if i >= 2:
                        pe.wait_ge(y_ready, i - 1)
                    for h4 in range(H4):
                        for b in range(UB):
                            ins = pe.matmul(ps_y[i % 2][QUAD * b:QUAD * b + QUAD, h4 * VW:(h4 + 1) * VW],
                                            PT[:, i % 2, b, h4 * S:(h4 + 1) * S], Vz[d][:, g * UB + b, h4, :],
                                            start=True, stop=True)
                    ins.then_inc(values_ready, 1)

        @block.scalar
        def _(act):
            act.dma_start(x_tok[:, 0:UH, :], x_dram[:, 0:UH, :]).then_inc(ld["x0"], 16)
            act.dma_start(x_tok[:, UH:G, :], x_dram[:, UH:G, :]).then_inc(ld["x1"], 16)
            act.dma_start(xT[:, :, :], xT_dram.rearrange("p (b s) -> p b s", s=S)).then_inc(ld["xT"], 16)
            act.wait_ge(ld["cols"], 16)
            act.activation(silu_t[:, 0, :], cols[:, R_COND:R_COND + B], ACT.Exp, scale=-1.0).then_inc(silu_e, 1)

            def take_part(name, part):
                ps = psum_of(name)
                act.wait_ge(dense_ready, DENSE.index(name) + 1)
                kind, h = (name, 0) if isinstance(name, str) else name[0:2]
                bs = slice(h * BH, (h + 1) * BH)
                if kind in ("q", "k"):
                    g0, g1 = STARTS[h]
                    bs = slice(g0 * UB, g1 * UB)
                    ps = ps[:, 0:(g1 - g0) * P]
                if kind == "k":
                    act.wait_ge(kz_ready, g0 // UH + 1)
                    for hq in (2 * part, 2 * part + 1):
                        q = slice(QUAD * hq, QUAD * hq + QUAD)
                        ins = act.activation(Kz[0][q, bs, hq, :], ps[q, :].rearrange("p (b k) -> p b k", k=S), ACT.Copy)
                    return ins
                if kind == "k1":
                    d = name[2]
                    if d == 1 and h == 0:
                        act.wait_ge(kz1_ready, 1)
                    for hq in (2 * part, 2 * part + 1):
                        q = slice(QUAD * hq, QUAD * hq + QUAD)
                        ins = act.activation(Kz[d][q, bs, hq, 0:M], ps[q, 0:BH * M].rearrange("p (b k) -> p b k", k=M),
                                             ACT.Identity, bias=cols[q, R_K + d:R_K + d + 1])
                    return ins
                if kind in ("v", "v1"):
                    d = name[2] if kind == "v1" else 0
                    nk = M if kind == "v1" else S
                    act.wait_ge(vz_ready[d], HQ * ((h + 1) if kind == "v" else 1 if d else HALVES))
                    for b in (part,):
                        for hq in range(HQ):
                            src = ps[QUAD * b:QUAD * b + nk, :].rearrange("p (u q h c) -> p u q h c", u=UH, q=HQ, h=H4)
                            ins = act.activation(
                                Vz[d][QUAD * hq:QUAD * hq + nk, h * BH + b:(h + 1) * BH:UB, :, hq * C:(hq + 1) * C],
                                src[:, :, hq, :, :], ACT.Copy)
                    return ins
                if kind == "qz":
                    return act.activation(qz[:, :], ps[:, 0:B], ACT.Copy)
                if kind == "yT":
                    return act.activation(yT[:, h * TH:(h + 1) * TH], ps[:, :], ACT.Copy)
                if kind == "mlp1":
                    j = name[2]
                    return act.activation(hidden[:, j, :], ps[:, :], ACT.Gelu_apprx_tanh,
                                          bias=cols[:, R_MLP1 + j:R_MLP1 + j + 1])
                if kind == "q":
                    act.wait_ge(masks_ready, 1)
                    return act.activation(Qm[0][:, bs, part, :], ps[:, :].rearrange("p (b q) -> p b q", q=S), ACT.Copy,
                                          scale=head_mask[:, 0, part:part + 1])
                if kind == "q1":
                    d, h4 = name[2], part
                    act.wait_ge(masks_ready, 2)
                    return act.activation(Qm[d][:, bs, h4, :], ps[:, :].rearrange("p (b q) -> p b q", q=S),
                                          ACT.Identity, scale=head_mask[:, 1, h4:h4 + 1],
                                          bias=bq_masked[:, d, h4:h4 + 1])
                assert kind == "out"
                g0, g1 = ENDS[h]
                return act.activation(out_tok[:, g0:g1, :], ps[:, 0:(g1 - g0) * P].rearrange("p (u f) -> p u f", f=P),
                                      ACT.Copy)

            for stage, i in ORDER:
                if stage == "take" and by_act(*i):
                    ins = take_part(*i)
                    if is_last_part(*i):
                        ins.then_inc(dense_act, 1)
                elif stage == "labels":
                    act.wait_ge(ld["adj"], 16)
                    gs = slice(i * G // LABEL_STEPS, (i + 1) * G // LABEL_STEPS)
                    act.activation(adj_f[:, gs, :, :].rearrange("p g j l -> p g (j l)"), adj_i[:, gs, :], ACT.Copy)\
                       .then_inc(adj_ready, 1)
                elif stage == "exp":
                    E, nk = (E1, M) if UNITS[i][0] else (E0, S)
                    act.wait_ge(*shift_of(i))
                    act.activation(E[:, i % 3, :, 0:nk], E[:, i % 3, :, 0:nk], ACT.Exp).then_inc(exp_ready, 1)
                elif stage == "copy":
                    act.wait_ge(turned, i + 1)
                    if i >= 2:
                        act.wait_ge(values_ready, i - 1)
                    act.activation(PT[:, i % 2, :, :], ps_t[:, :].rearrange("p (b t) -> p b t", t=P), ACT.Copy)\
                       .then_inc(pt_ready, 1)

        @block.vector
        def _(dve):
            count = [0]

            def wait_own(ins):
                count[0] += 1
                ins.then_inc(own, 1)
                dve.wait_ge(own, count[0])

            def norm_stats(layer, g0, g1, src):
                for g in range(g0, g1):
                    ins = dve.bn_stats(stats[:, g, :], src(g))
                wait_own(ins)
                for g in range(g0, g1):
                    ins = dve.bn_aggr(meanvar[:, g, :], stats[:, g, :])
                wait_own(ins)
                dve.tensor_scalar(var_eps[:, g0:g1], meanvar[:, g0:g1, 1], LN_EPS, None, ALU.add).then_inc(var_ready, 1)

            def norm_apply(layer, g0, g1, src):
                dve.wait_ge(rstd_ready, rstd_count(layer, g0))
                for g in range(g0, g1):
                    ins = dve.tensor_scalar(xn_tok[:, g, :], src(g), meanvar[:, g, 0:1], rstd[:, layer, g:g + 1],
                                            ALU.subtract, ALU.mult)
                return ins

            def modulate(dst, ps, shift, scale, bs):
                wait_own(dve.tensor_tensor(dst[:, bs, :], ps[:, :].rearrange("p (b s) -> p b s", s=S),
                                           cmod[:, scale, bs].unsqueeze(2).broadcast_to([P, bs.stop - bs.start, S]),
                                           ALU.mult))
                return dve.tensor_tensor(dst[:, bs, :], dst[:, bs, :],
                                         cmod[:, shift, bs].unsqueeze(2).broadcast_to([P, bs.stop - bs.start, S]),
                                         ALU.add)

            def gated_residual(dst, ps, bias, gate, res, bs):
                ins = dve.scalar_tensor_tensor(out=gated[:, bs, :], in0=ps[:, :].rearrange("p (b s) -> p b s", s=S),
                                               scalar=cols[:, bias:bias + 1],
                                               in1=cmod[:, gate, bs].unsqueeze(2).broadcast_to([P, BH, S]),
                                               op0=ALU.add, op1=ALU.mult)
                ins.then_inc(dense_dve, 1)
                dve.wait_ge(dense_dve, dve_taken[0] + 1)
                return dve.tensor_tensor(dst[:, bs, :], gated[:, bs, :], res[:, bs, :], ALU.add)

            dve_taken = [0]

            def silu():
                dve.wait_ge(silu_e, 1)
                wait_own(dve.tensor_scalar(silu_t[:, 1, :], silu_t[:, 0, :], 1.0, None, ALU.add))
                wait_own(dve.reciprocal(silu_t[:, 0, :], silu_t[:, 1, :]))
                dve.tensor_tensor(silu_c[:, :], silu_t[:, 0, :], cols[:, R_COND:R_COND + B], ALU.mult)\
                   .then_inc(silu_ready, 1)
                for j in (1, 4):
                    ins = dve.tensor_scalar(cols[:, R_ADA + j:R_ADA + j + 1], cols[:, R_ADA + j:R_ADA + j + 1], 1.0,
                                            None, ALU.add)
                wait_own(ins)

            def graph_biases():
                dve.tensor_tensor(bout_sum[:, :], cols[:, R_OUT:R_OUT + 1], cols[:, R_OUT + 1:R_OUT + 2], ALU.add)
                for d in range(DIRS):
                    ins = dve.tensor_scalar(bq_masked[:, d, :], head_mask[:, 1, :], cols[:, R_Q + d:R_Q + d + 1], None,
                                            ALU.mult)
                ins.then_inc(masks_ready, 1)

            def head_masks():
                dve.wait_ge(ident_ready, 1)
                wait_own(dve.tensor_reduce(head_mask[:, 2, :],
                                           ident[:, :].rearrange("p (q h c) -> p h q c", q=HQ, h=H4), AX.XY, ALU.add))
                dve.tensor_scalar(head_mask[:, 1, :], head_mask[:, 2, :], C ** -0.5, None, ALU.mult)
                dve.tensor_scalar(head_mask[:, 0, :], head_mask[:, 2, :], 1.0 / C, None, ALU.mult)\
                   .then_inc(masks_ready, 1)
                dve.wait_ge(masks_ready, 1)

            def edge_bias():
                dve.wait_ge(labels_ready, 1)
                wait_own(dve.tensor_scalar(masked[:, :, :], label_sum[:, :, :], 0.0, NEG, ALU.is_le, ALU.mult))
                dve.scalar_tensor_tensor(out=bias_dir[:, 0, :, :], in0=label_bias[:, :, :], scalar=bb[:, 0:1],
                                         in1=masked[:, :, :], op0=ALU.add, op1=ALU.add).then_inc(bias_ready, 1)
                dve.wait_ge(bias_ready, 1)
                dve.transpose(bias_dir[:, 1, :, :], bias_dir[:, 0, :, :]).then_inc(bias_ready, 1)

            def take_part(name, part):
                ps = psum_of(name)
                dve.wait_ge(dense_ready, DENSE.index(name) + 1)
                kind, h = (name, 0) if isinstance(name, str) else name[0:2]
                bs = slice(h * BH, (h + 1) * BH)
                if kind in ("xnT", "q", "k"):
                    g0, g1 = STARTS[h]
                    bs = slice(g0 * UB, g1 * UB)
                    ps = ps[:, 0:(g1 - g0) * P]
                ps_bs = ps[:, :].rearrange("p (b s) -> p b s", s=S)
                if kind == "cmod":
                    j0, j1 = ADA_CHUNKS[h]
                    dve.tensor_tensor(cmod[:, j0:j1, :], ps[:, j0 * B:j1 * B].rearrange("p (j b) -> p j b", b=B),
                                      cols[:, R_ADA + j0:R_ADA + j1].unsqueeze(2).broadcast_to([P, j1 - j0, B]),
                                      ALU.add)\
                       .then_inc(dense_dve, 1)
                    dve.wait_ge(dense_dve, dve_taken[0] + 1)
                elif kind == "xnT":
                    modulate(xm, ps, 0, 1, bs).then_inc(dense_dve, 1)
                elif kind == "q":
                    ins = dve.tensor_scalar(Qm[0][:, bs, part, :], ps_bs, head_mask[:, 0, part:part + 1], None,
                                            ALU.mult)
                    if is_last_part(name, part):
                        ins.then_inc(dense_dve, 1)
                elif kind == "proj":
                    if h == 0:
                        dve.wait_ge(ld["xT"], 16)
                    gated_residual(x1T, ps, R_PROJ, 2, xT, bs).then_inc(x1_ready, 1)
                elif kind == "x1tok":
                    g0, g1 = h * UH, (h + 1) * UH
                    if part == 0:
                        norm_stats(1, g0, g1, lambda g: ps[:, (g - g0) * P:(g - g0 + 1) * P])
                    else:
                        norm_apply(1, g0, g1, lambda g: ps[:, (g - g0) * P:(g - g0 + 1) * P]).then_inc(dense_dve, 1)
                elif kind == "xn2T":
                    modulate(xm2, ps, 3, 4, bs).then_inc(dense_dve, 1)
                elif kind == "mlp2":
                    dve.wait_ge(x1_ready, h + 1)
                    gated_residual(x2T, ps, R_MLP2, 5, x1T, bs).then_inc(x2_ready, 1)
                elif kind == "rowsum":
                    wait_taken(dve, "qz")
                    dve.scalar_tensor_tensor(out=zeroed_q[:, :, :], in0=ps_bs, scalar=0.0,
                                             in1=qz[:, bs].unsqueeze(2).broadcast_to([P, BH, S]),
                                             op0=ALU.not_equal, op1=ALU.mult).then_inc(dense_dve, 1)
                    dve.wait_ge(dense_dve, dve_taken[0] + 1)
                elif kind == "self":
                    dve.scalar_tensor_tensor(out=selfT[:, bs, :], in0=ps_bs, scalar=cols[:, R_SELF:R_SELF + 1],
                                             in1=zeroed_q[:, :, :], op0=ALU.add, op1=ALU.add).then_inc(dense_dve, 1)
                elif kind in ("k", "k1"):
                    d, nk = (0, S) if kind == "k" else (name[2], M)
                    if kind == "k":
                        dve.wait_ge(kz_ready, g0 // UH + 1)
                    elif d == 1:
                        dve.wait_ge(kz1_ready, 1)
                    for hq in (2 * part, 2 * part + 1):
                        qs = slice(QUAD * hq, QUAD * hq + QUAD)
                        src = ps[qs, 0:(bs.stop - bs.start) * nk].rearrange("p (b k) -> p b k", k=nk)
                        dst = Kz[d][qs, bs, hq, 0:nk]
                        if kind == "k":
                            ins = dve.tensor_copy(dst, src)
                        else:
                            ins = dve.tensor_scalar(dst, src, cols[qs, R_K + d:R_K + d + 1], None, ALU.add)
                    if is_last_part(name, part):
                        ins.then_inc(dense_dve, 1)
                elif kind == "q1":
                    d = name[2]
                    ins = dve.tensor_scalar(Qm[d][:, bs, part, :], ps_bs, cols[:, R_Q + d:R_Q + d + 1],
                                            head_mask[:, 1, part:part + 1], ALU.add, ALU.mult)
                    if is_last_part(name, part):
                        ins.then_inc(dense_dve, 1)
                else:
                    assert kind == "yfT"
                    g0, g1 = ENDS[h]
                    bs = slice(g0 * UB, g1 * UB)
                    ps_bs = ps_bs[:, 0:(g1 - g0) * UB, :]
                    dve.scalar_tensor_tensor(out=rT[:, bs, :], in0=ps_bs, scalar=bout_sum[:, 0:1], in1=selfT[:, bs, :],
                                             op0=ALU.add, op1=ALU.add).then_inc(dense_dve, 1)
                    dve.wait_ge(dense_dve, dve_taken[0] + 1)
                    dve.scalar_tensor_tensor(out=outT[:, bs, :], in0=rT[:, bs, :], scalar=0.0, in1=x2T[:, bs, :],
                                             op0=ALU.max, op1=ALU.add).then_inc(outT_ready, 1)
                if is_last_part(name, part):
                    dve_taken[0] += 1

            def softmax_steps(n, m):
                if n is not None:
                    layer, d, g = UNITS[n]
                    nm = neg_max[:, n % 3, :]
                    dve.wait_ge(scores_ready, n + 1)
                    if n >= 3:
                        dve.wait_ge(turned, n - 2)
                    if layer:
                        if n == N0:
                            dve.wait_ge(bias_spread, 16 * H4)
                        e = sc = E1[:, n % 3, :, 0:M]
                        dve.tensor_tensor(e.rearrange("p (b q) k -> p b q k", b=UB),
                                          ps_s[n % 2][:, :].rearrange("p (b r) -> p b r", b=UB)[:, :, 0:HQ * M]
                                          .rearrange("p b (q k) -> p b q k", k=M),
                                          bias_rep[:, d, g * UB:(g + 1) * UB, :].unsqueeze(2)
                                          .broadcast_to([P, UB, HQ, M]), ALU.add).then_inc(scores_read, 1)
                    else:
                        e = E0[:, n % 3, :, :]
                        sc = ps_s[n % 2][:, :].rearrange("p (j k) -> p j k", k=S)
                        dve.tensor_reduce(nm, sc, AX.X, ALU.max, negate=True).then_inc(max_ready, 1)
                if m is not None:
                    dve.wait_ge(values_ready, m + 1)
                    yv = ps_y[m % 2][:, 0:H4 * VW].rearrange("p (h w) -> p h w", w=VW)
                    dve.reciprocal(rden[:, m % 2, :, :], yv[:, :, HQ * C:VW]).then_inc(rden_ready, 1)
                if n is not None and layer:
                    dve.wait_ge(scores_read, n + 1 - N0)
                    dve.tensor_reduce(nm, sc, AX.X, ALU.max, negate=True).then_inc(max_ready, 1)
                if m is not None:
                    m_layer, m_d, m_g = UNITS[m]
                    dst = y_dir[m_d][:, m_g, :] if m_layer else y_tok[:, m_g, :]
                    dve.wait_ge(rden_ready, m + 1)
                    dve.tensor_tensor(dst.rearrange("p (q h c) -> p h q c", q=HQ, h=H4),
                                      yv[:, :, 0:HQ * C].rearrange("p h (q c) -> p h q c", c=C),
                                      rden[:, m % 2, :, :].unsqueeze(3).broadcast_to([P, H4, HQ, C]), ALU.mult)\
                       .then_inc(y_ready, 1)
                if n is not None and n not in POOL_SUBS:
                    dve.wait_ge(max_ready, n + 1)
                    dve.tensor_tensor(e, sc, nm.unsqueeze(2).broadcast_to([P, UB * HQ, sc.shape[2]]), ALU.add)\
                       .then_inc(shifted, 1)
                if m is not None and m_layer and m_d == 1 and m_g + 1 in [g1 for g0, g1 in ENDS]:
                    gs = slice(*[ends for ends in ENDS if ends[1] == m_g + 1][0])
                    dve.wait_ge(y_ready, m + 1)
                    dve.tensor_tensor(y_dir[0][:, gs, :], y_dir[0][:, gs, :], y_dir[1][:, gs, :], ALU.add)\
                       .then_inc(ysum_ready, 1)

            dve.memset(Kz[0][:, 0:BH, :, :], 0.0).then_inc(kz_ready, 1)
            dve.wait_ge(ld["x0"], 16)
            norm_stats(0, *STARTS[0], lambda g: x_tok[:, g, :])
            silu()
            norm_apply(0, *STARTS[0], lambda g: x_tok[:, g, :]).then_inc(xn_ready, 1)
            head_masks()
            for stage, i in ORDER:
                if stage == "take" and not by_act(*i):
                    take_part(*i)
                elif stage == "norm1":
                    c, step = i
                    if step == 0:
                        if STARTS[c][1] > UH:
                            dve.wait_ge(ld["x1"], 16)
                        norm_stats(0, *STARTS[c], lambda g: x_tok[:, g, :])
                        if c == len(STARTS) - 1:
                            graph_biases()
                    else:
                        norm_apply(0, *STARTS[c], lambda g: x_tok[:, g, :]).then_inc(xn_ready, 1)
                elif stage == "edges":
                    edge_bias()
                elif stage == "soft":
                    softmax_steps(*i)


def kernel(**inputs):
    import numpy as np
    import concourse.bacc as bacc
    from concourse.bass_utils import run_bass_kernel_spmd

    a = {name: np.asarray(value) for name, value in inputs.items()}
    vectors = [a["cond_1024"]] + [a[n].reshape(-1, P) for n in (
        "L0_cond_b_ada", "L0_cond_b_proj", "L0_cond_b_mlp1", "L0_cond_b_mlp2", "L1_cond_b_self", "L1_cond_bq",
        "L1_cond_bk", "L1_cond_bout")]
    cols = np.concatenate([np.concatenate(vectors).T, np.broadcast_to(a["L1_cond_w_bias"], (P, L)),
                           np.broadcast_to(a["L1_cond_b_bias"], (P, 1))], axis=1)
    x = a["x"]
    w_graph = [a["L1_cond_W_self"].T.reshape(2, P, P)] + [
        a[n].reshape(DIRS, P, P).transpose(0, 2, 1) for n in ("L1_cond_Wq", "L1_cond_Wk", "L1_cond_Wout")]
    arrays = {
        "cols": cols,
        "x_tok": x.reshape(G, UB * S, P).transpose(1, 0, 2),
        "xT": x.reshape(B * S, P).T,
        "adj": a["mask_BxSxSx11_ik0"].reshape(G, UB * S, S * L).transpose(1, 0, 2),
        "w_ada": a["L0_cond_w_ada"],
        "w_qkv": a["L0_cond_w_qkv"],
        "w_rest": np.concatenate([a["L0_cond_w_proj"], a["L0_cond_w_mlp1"],
                                  a["L0_cond_w_mlp2"].reshape(NJ, P, P).transpose(1, 0, 2).reshape(P, NJ * P)]
                                 + [w for ws in w_graph for w in ws], axis=1),
    }
    arrays = {name: np.ascontiguousarray(value) for name, value in arrays.items()}
    nc = bacc.Bacc("TRN2", target_bir_lowering=False, num_devices=1)
    ins = {name: nc.dram_tensor("in_" + name, value.shape, mybir.dt.from_np(value.dtype), kind="ExternalInput").ap()
           for name, value in arrays.items()}
    out = nc.dram_tensor("out_0", (B, S, P), F32, kind="ExternalOutput").ap()
    program(nc, out=out, **ins)
    r = run_bass_kernel_spmd(nc, [{"in_" + name: value for name, value in arrays.items()}], core_ids=[0])
    return r.results[0]["out_0"]
```
